# Optimizing a Trainium2 kernel written in Bass

```python
import numpy as np
import jax
import jax.numpy as jnp

def _softmax(x, axis=-1):
    return jax.nn.softmax(x, axis=axis)

def _gelu(x):
    return jax.nn.gelu(x, approximate=True)

def _silu(x):
    return jax.nn.silu(x)

def _sigmoid(x):
    return jax.nn.sigmoid(x)

def _layernorm(x, axis=-1, eps=1e-05):
    m = jnp.mean(x, axis=axis, keepdims=True)
    v = jnp.var(x, axis=axis, keepdims=True)
    return (x - m) / jnp.sqrt(v + eps)

def _scatter_add(tgt, idx, src, axis=0):
    return tgt.at[idx].add(src)

def _segment_sum(src, seg, n):
    return jax.ops.segment_sum(src, seg, n)
kernel_name = 'mk_macaron_d1_jaxref_r4_d79e43'

def setup_inputs(seed: int=0):
    np.random.seed(seed)
    _w = jnp.asarray

    def _L0_attn_setup():
        import jax, jax.numpy as jnp
        import numpy as np
        N_HEAD = 16
        PAGE_SIZE = 64
        ROPE_THETA = 10000.0

        def _rope_tables(T, D, dtype):
            inv = 1.0 / ROPE_THETA ** (np.arange(0, D, 2, dtype=np.float32) / D)
            ang = np.outer(np.arange(T, dtype=np.float32), inv)
            return (jnp.asarray(np.cos(ang), dtype), jnp.asarray(np.sin(ang), dtype))

        def _apply_rope(x, cos, sin):
            x1 = x[..., 0::2]
            x2 = x[..., 1::2]
            c = cos[None, :, None, :]
            s = sin[None, :, None, :]
            out = jnp.stack([x1 * c - x2 * s, x1 * s + x2 * c], axis=-1)
            return out.reshape(x.shape)
        key = jax.random.key(seed)
        ks = jax.random.split(key, 6)
        B, T, E = (2, 512, 256)
        L = E // 2
        sc = lambda fan: 1.0 / np.sqrt(fan)
        return {'x': jax.random.normal(ks[0], (B, T, E), jnp.float32), 'wq': jax.random.normal(ks[1], (E, E), jnp.float32) * sc(E), 'w_down': jax.random.normal(ks[2], (E, L), jnp.float32) * sc(E), 'wk_up': jax.random.normal(ks[3], (L, E), jnp.float32) * sc(L), 'wv_up': jax.random.normal(ks[4], (L, E), jnp.float32) * sc(L), 'wo': jax.random.normal(ks[5], (E, E), jnp.float32) * sc(E)}
    _L0_attn_in = _L0_attn_setup()

    def _L0_ffn_setup():
        import jax, jax.numpy as jnp
        import numpy as np
        E = 64
        K = 6
        CAP = 128
        ROUTE_SCALE = 1.0
        key = jax.random.key(seed)
        ks = jax.random.split(key, 9)
        B, S, D, I = (2, 256, 256, 176)
        SI = 2 * I
        s = 0.02
        return {'x': jax.random.normal(ks[0], (B, S, D), jnp.float32), 'gate_w': jax.random.normal(ks[1], (E, D), jnp.float32) * s, 'gate_b': jnp.zeros((E,), jnp.float32), 'w1': jax.random.normal(ks[2], (E, I, D), jnp.float32) * s, 'w2': jax.random.normal(ks[3], (E, D, I), jnp.float32) * s, 'w3': jax.random.normal(ks[4], (E, I, D), jnp.float32) * s, 'ws1': jax.random.normal(ks[5], (SI, D), jnp.float32) * s, 'ws2': jax.random.normal(ks[6], (D, SI), jnp.float32) * s, 'ws3': jax.random.normal(ks[7], (SI, D), jnp.float32) * s}
    _L0_ffn_in = _L0_ffn_setup()
    _d = {'L0_attn_x': _L0_attn_in['x'], 'L0_attn_wq': _L0_attn_in['wq'], 'L0_attn_w_down': _L0_attn_in['w_down'], 'L0_attn_wk_up': _L0_attn_in['wk_up'], 'L0_attn_wv_up': _L0_attn_in['wv_up'], 'L0_attn_wo': _L0_attn_in['wo'], 'L0_ffn_gate_w': _L0_ffn_in['gate_w'], 'L0_ffn_gate_b': _L0_ffn_in['gate_b'], 'L0_ffn_w1': _L0_ffn_in['w1'], 'L0_ffn_w2': _L0_ffn_in['w2'], 'L0_ffn_w3': _L0_ffn_in['w3'], 'L0_ffn_ws1': _L0_ffn_in['ws1'], 'L0_ffn_ws2': _L0_ffn_in['ws2'], 'L0_ffn_ws3': _L0_ffn_in['ws3']}
    _x0 = _d['L0_attn_x']
    _d['L0_attn_x'] = jax.random.normal(jax.random.fold_in(jax.random.key(seed), 1), (16, 512, 256), dtype=_x0.dtype)
    del _x0
    return _d

def reference(L0_attn_x, L0_attn_wq, L0_attn_w_down, L0_attn_wk_up, L0_attn_wv_up, L0_attn_wo, L0_ffn_gate_w, L0_ffn_gate_b, L0_ffn_w1, L0_ffn_w2, L0_ffn_w3, L0_ffn_ws1, L0_ffn_ws2, L0_ffn_ws3):

    def _L0_attn_ref(x, wq, w_down, wk_up, wv_up, wo):
        import jax, jax.numpy as jnp
        import numpy as np
        N_HEAD = 16
        PAGE_SIZE = 64
        ROPE_THETA = 10000.0

        def _rope_tables(T, D, dtype):
            inv = 1.0 / ROPE_THETA ** (np.arange(0, D, 2, dtype=np.float32) / D)
            ang = np.outer(np.arange(T, dtype=np.float32), inv)
            return (jnp.asarray(np.cos(ang), dtype), jnp.asarray(np.sin(ang), dtype))

        def _apply_rope(x, cos, sin):
            x1 = x[..., 0::2]
            x2 = x[..., 1::2]
            c = cos[None, :, None, :]
            s = sin[None, :, None, :]
            out = jnp.stack([x1 * c - x2 * s, x1 * s + x2 * c], axis=-1)
            return out.reshape(x.shape)
        B, T, E = x.shape
        H = N_HEAD
        D = E // H
        q = (x @ wq).reshape(B, T, H, D)
        lat = x @ w_down
        k = (lat @ wk_up).reshape(B, T, H, D)
        v = (lat @ wv_up).reshape(B, T, H, D)
        cos, sin = _rope_tables(T, D, x.dtype)
        q = _apply_rope(q, cos, sin)
        k = _apply_rope(k, cos, sin)
        scale = 1.0 / jnp.sqrt(jnp.asarray(D, x.dtype))
        scores = jnp.einsum('bqhd,bkhd->bhqk', q, k) * scale
        pages = jnp.arange(T) // PAGE_SIZE
        allowed = pages[None, :] <= pages[:, None]
        scores = jnp.where(allowed[None, None], scores, jnp.finfo(scores.dtype).min)
        attn = jax.nn.softmax(scores, axis=-1)
        out = jnp.einsum('bhqk,bkhd->bqhd', attn, v).reshape(B, T, E)
        return out @ wo

    def _L0_ffn_ref(x, gate_w, gate_b, w1, w2, w3, ws1, ws2, ws3):
        import jax, jax.numpy as jnp
        import numpy as np
        E = 64
        K = 6
        CAP = 128
        ROUTE_SCALE = 1.0
        shape = x.shape
        D = shape[-1]
        xf = x.reshape(-1, D)
        T = xf.shape[0]
        scores = jax.nn.softmax(xf @ gate_w.T, axis=-1)
        _, idx = jax.lax.top_k(scores + gate_b, K)
        weights = jnp.take_along_axis(scores, idx, axis=1) * ROUTE_SCALE
        flat_e = idx.reshape(-1)
        order = jnp.argsort(flat_e)
        se = flat_e[order]
        counts = jnp.bincount(flat_e, length=E)
        starts = jnp.cumsum(counts) - counts
        pos = jnp.arange(T * K) - starts[se]
        tok = order // K
        xb = jnp.zeros((E, CAP, D), xf.dtype).at[se, pos].set(xf[tok], mode='drop')
        h = jax.nn.silu(jnp.einsum('ecd,eid->eci', xb, w1)) * jnp.einsum('ecd,eid->eci', xb, w3)
        yb = jnp.einsum('eci,edi->ecd', h, w2)
        valid = (pos < CAP).astype(xf.dtype)
        contrib = yb[se, jnp.minimum(pos, CAP - 1)]
        wf = weights.reshape(-1)[order] * valid
        y = jnp.zeros_like(xf).at[tok].add(contrib * wf[:, None])
        z = jax.nn.silu(xf @ ws1.T) * (xf @ ws3.T) @ ws2.T
        return (y + z).reshape(shape)
    x = L0_attn_x
    x = x + 0.5 * _L0_ffn_ref(_layernorm(x, axis=-1), L0_ffn_gate_w, L0_ffn_gate_b, L0_ffn_w1, L0_ffn_w2, L0_ffn_w3, L0_ffn_ws1, L0_ffn_ws2, L0_ffn_ws3)
    x = x + _L0_attn_ref(_layernorm(x, axis=-1), L0_attn_wq, L0_attn_w_down, L0_attn_wk_up, L0_attn_wv_up, L0_attn_wo)
    x = x + 0.5 * _L0_ffn_ref(_layernorm(x, axis=-1), L0_ffn_gate_w, L0_ffn_gate_b, L0_ffn_w1, L0_ffn_w2, L0_ffn_w3, L0_ffn_ws1, L0_ffn_ws2, L0_ffn_ws3)
    return x

_drawn_inputs = setup_inputs


def setup_inputs(seed=0):
    import zlib

    import numpy as np

    out = dict(_drawn_inputs(seed))
    spreads = {'L0_ffn_gate_b': (0.0, 0.8)}
    factors = {'L0_ffn_gate_w': 8.0,
     'L0_ffn_w1': 8.0,
     'L0_ffn_w2': 8.0,
     'L0_ffn_w3': 8.0,
     'L0_ffn_ws1': 2.898,
     'L0_ffn_ws2': 2.871,
     'L0_ffn_ws3': 2.868}
    for name, (base, spread) in spreads.items():
        noise = np.random.default_rng([zlib.crc32(name.encode()), seed]).standard_normal(out[name].shape)
        drawn = base * np.exp(spread * noise) if base else spread * noise
        out[name] = jnp.asarray(drawn.astype(out[name].dtype))
    for name, factor in factors.items():
        out[name] = (out[name] * factor).astype(out[name].dtype)
    return out
```

```python
import concourse.bass as bass
from concourse import mybir
from contextlib import ExitStack

F32 = mybir.dt.float32
BF16 = mybir.dt.bfloat16
I32 = mybir.dt.int32
U32 = mybir.dt.uint32
ALU = mybir.AluOpType
ACT = mybir.ActivationFunctionType
AX = mybir.AxisListType

P = 128
B, T, D = 16, 512, 256
TOK = B * T
NT = T // P
DC = D // P
E, K, CAP = 64, 6, 128
I = 176
IH = I // 2
SI = 2 * I
SJ = [128, 128, SI - 256]
ROW = D + E
DUMMY = TOK
H, HD = 16, 16
EPS = 1e-5
RING = 2


def token_stats(nc, dve, x, stats, mv):
    for t in range(NT):
        nc.vector.bn_stats(stats[:, t, :], x[:, t, :])
    dve.drain()
    for t in range(NT):
        last = nc.vector.bn_aggr(mv[:, t, :], stats[:, t, :])
    return last


def token_scales(nc, pool, mv, rstd, shift, w):
    nc.gpsimd.tensor_tensor(rstd[:], mv[:, :, 1], w.eps[:], ALU.add)
    nc.gpsimd.tensor_tensor(shift[:], mv[:, :, 0], w.minus_one[:], ALU.mult)
    pool.drain()
    nc.gpsimd.tensor_tensor(rstd[:], rstd[:], w.minus_half[:], ALU.pow)
    pool.drain()
    return nc.gpsimd.tensor_tensor(shift[:], shift[:], rstd[:], ALU.mult)


def token_normalise(nc, x, rstd, shift, xn):
    for t in range(NT):
        last = nc.scalar.activation(xn[:, t, 0:D], x[:, t, :], ACT.Identity, bias=shift[:, t:t + 1],
                                    scale=rstd[:, t:t + 1])
    return last


def route_and_share(nc, w, dram, src, acc, tag):
    N = B
    with ExitStack() as ctx:
        def sb(name, shape, dt=F32):
            return ctx.enter_context(nc.sbuf_tensor(f"{tag}_{name}", shape, dt))

        def ps(name, shape, dt=F32):
            return ctx.enter_context(nc.psum_tensor(f"{tag}_{name}", shape, dt))

        def sem(name):
            return ctx.enter_context(nc.semaphore(f"{tag}_{name}"))

        ws1T, ws3T = sb("ws1T", [P, DC, SI]), sb("ws3T", [P, DC, SI])
        ws2T = sb("ws2T", [P, 3, D])
        x = [sb(f"x{u}", [P, NT, D]) for u in range(2)]
        row = [sb(f"row{u}", [P, NT, ROW]) for u in range(2)]
        stats = sb("stats", [P, NT, 6])
        mv = sb("mv", [P, NT, 2])
        rstd = sb("rstd", [P, NT])
        shift = sb("shift", [P, NT])
        xnT = sb("xnT", [P, DC, T])
        gmax = sb("gmax", [P, NT])
        shifted = sb("shifted", [P, NT, E])
        expd = sb("expd", [P, NT, E])
        gsum = sb("gsum", [P, NT])
        grec = sb("grec", [P, NT])
        biased = sb("biased", [P, NT, E])
        top = sb("top", [P, NT, 8])
        topi = sb("topi", [P, NT, 8], U32)
        topf = sb("topf", [P, NT, K])
        pick = sb("pick", [P, NT, K, E], BF16)
        picked = sb("picked", [P, NT, E], BF16)
        earlier = sb("earlier", [P, E], BF16)
        newer = sb("newer", [P, E])
        prod = sb("prod", [P, NT, K, E])
        rank = sb("rank", [P, NT, K])
        at_slot = sb("at_slot", [P, NT, K, CAP], BF16)
        who = sb("who", [P, NT, K, 2, E], BF16)
        tile_no = sb("tile_no", [P, NT])
        silu = [sb(f"silu{n}", [P, T]) for n in range(RING)]
        hidden = [sb(f"hidden{j}", [P, T]) for j in range(3)]
        table = sb("table", [P, 2, E])
        empty = sb("empty", [P, E])
        zero = sb("zero", [P, P], BF16)

        p_turn = ps("p_turn", [P, T])
        p_gate = ps("p_gate", [P, 2, NT, E])
        p_table = ps("p_table", [P, T])
        p_up = [[ps(f"p_up{n}{g}", [P, T]) for g in range(2)] for n in range(RING)]
        p_z = ps("p_z", [P, 2, D])

        x_loaded = [sem(f"x_loaded{u}") for u in range(2)]
        acc_stored = [sem(f"acc_stored{u}") for u in range(2)]
        rows_stored = [sem(f"rows_stored{u}") for u in range(2)]
        shared_loaded = sem("shared_loaded")
        stats_ready = sem("stats_ready")
        scales_ready = sem("scales_ready")
        xn_ready = sem("xn_ready")
        turned = sem("turned")
        xnT_ready = sem("xnT_ready")
        logits_ready = sem("logits_ready")
        shifted_ready = sem("shifted_ready")
        exp_ready = sem("exp_ready")
        probs_ready = sem("probs_ready")
        picked_ready = sem("picked_ready")
        ranks_ready = sem("ranks_ready")
        onehots_ready = sem("onehots_ready")
        table_added = sem("table_added")
        up_ready = sem("up_ready")
        silu_ready = sem("silu_ready")
        hidden_ready = sem("hidden_ready")
        z_ready = sem("z_ready")
        acc_ready = sem("acc_ready")
        setup_done = sem("setup_done")

        def loop(eng, chunk):
            with eng.Fori(0, N // 2 - 1) as i:
                for u in range(2):
                    chunk(2 * i + u, i, u, False)
            chunk(N - 2, N // 2 - 1, 0, False)
            chunk(N - 1, N // 2 - 1, 1, True)

        with nc.Block() as block:
            @block.sync
            def _(sp):
                sp.dma_start(x[0][:], src[0]).then_inc(x_loaded[0], 16)
                sp.dma_start(ws1T[:], dram.ws1T).then_inc(shared_loaded, 16)
                sp.dma_start(ws3T[:], dram.ws3T).then_inc(shared_loaded, 16)
                for j in range(3):
                    sp.dma_start(ws2T[0:SJ[j], j, :], dram.ws2T[j * P:j * P + SJ[j], :]).then_inc(shared_loaded, 16)

                def chunk(c, i, u, last):
                    if not last:
                        if u == 0:
                            sp.wait_ge(acc_stored[1], 16 * i)
                            sp.dma_start(x[1][:], src[c + 1]).then_inc(x_loaded[1], 16)
                        else:
                            sp.wait_ge(acc_stored[0], 16 * i + 16)
                            sp.dma_start(x[0][:], src[c + 1]).then_inc(x_loaded[0], 16)
                    sp.wait_ge(xn_ready, c + 1)
                    sp.wait_ge(probs_ready, c + 1)
                    sp.dma_start(dram.rows_chunks[c], row[u][:]).then_inc(rows_stored[u], 16)
                    sp.wait_ge(acc_ready, 2 * c + 2)
                    sp.dma_start(acc[c], x[u][:]).then_inc(acc_stored[u], 16)

                loop(sp, chunk)
                for u in range(2):
                    sp.wait_ge(acc_stored[u], 8 * N)
                    sp.wait_ge(rows_stored[u], 8 * N)

            @block.gpsimd
            def _(pool):
                def scales(c):
                    pool.wait_ge(xn_ready, c)
                    pool.wait_ge(stats_ready, c + 1)
                    token_scales(nc, pool, mv, rstd, shift, w).then_inc(scales_ready, 1)

                scales(0)
                with pool.Fori(1, N) as c:
                    scales(c)

            @block.scalar
            def _(act):
                def evacuate(c):
                    for h in range(DC):
                        act.wait_ge(turned, DC * c + h + 1)
                        nc.scalar.copy(xnT[:, h, :], p_turn[:]).then_inc(xnT_ready, 1)

                def normalise(c, i, u):
                    act.wait_ge(rows_stored[u], 16 * i)
                    act.wait_ge(scales_ready, c + 1)
                    token_normalise(nc, x[u], rstd, shift, row[u]).then_inc(xn_ready, 1)

                normalise(0, 0, 0)
                evacuate(0)

                def chunk(c, i, u, last):
                    act.wait_ge(shifted_ready, c + 1)
                    nc.scalar.activation(expd[:], shifted[:], ACT.Exp).then_inc(exp_ready, 1)
                    for j in range(3):
                        n = (u + j) % RING
                        m = SJ[j]
                        act.wait_ge(hidden_ready, 3 * c + j + 1)
                        act.wait_ge(up_ready, 3 * c + j + 1)
                        nc.scalar.activation(silu[n][0:m, :], p_up[n][0][0:m, :], ACT.Silu).then_inc(silu_ready, 1)
                        if j == 0 and not last:
                            normalise(c + 1, i + u, 1 - u)
                    if not last:
                        evacuate(c + 1)

                loop(act, chunk)

            @block.vector
            def _(dve):
                nc.vector.memset(earlier[:], 0.0)
                nc.vector.memset(zero[:], 0.0)
                nc.vector.tensor_copy(tile_no[:], w.first_tiles[:])
                dve.drain()
                dve.sem_inc(hidden_ready, RING)
                dve.sem_inc(setup_done, 1)

                def statistics(c, i, u):
                    dve.wait_ge(x_loaded[u], 16 * i + 16)
                    dve.wait_ge(scales_ready, c)
                    token_stats(nc, dve, x[u], stats, mv).then_inc(stats_ready, 1)

                def multiply(c, u, j):
                    n = (u + j) % RING
                    m = SJ[j]
                    dve.wait_ge(silu_ready, 3 * c + j + 1)
                    nc.vector.tensor_tensor(hidden[j][0:m, :], silu[n][0:m, :], p_up[n][1][0:m, :],
                                            ALU.mult).then_inc(hidden_ready, 1)

                def onehots(c):
                    dve.wait_ge(table_added, c)
                    nc.vector.tensor_tensor(tile_no[:], tile_no[:], w.tiles_per_chunk[:], ALU.add)
                    dve.drain()
                    for t in range(NT):
                        for k in range(K):
                            nc.vector.tensor_scalar(at_slot[:, t, k, :], w.iota_slot[:], rank[:, t, k:k + 1],
                                                    None, ALU.is_equal)
                    nc.vector.tensor_scalar(who[:, :, :, 0, :].rearrange("p t k e -> p (t k) e"),
                                            pick[:].rearrange("p t k e -> p (t k) e"), w.lane[:, 0:1],
                                            None, ALU.mult)
                    for t in range(NT):
                        ins = nc.vector.tensor_scalar(who[:, t, :, 1, :], pick[:, t, :, :], tile_no[:, t:t + 1],
                                                      None, ALU.mult)
                    ins.then_inc(onehots_ready, 1)

                statistics(0, 0, 0)

                def chunk(c, i, u, last):
                    dve.wait_ge(logits_ready, c + 1)
                    nc.vector.tensor_reduce(gmax[:], p_gate[:, 0, :, :], AX.X, ALU.max)
                    dve.drain()
                    nc.vector.tensor_tensor(shifted[:], p_gate[:, 0, :, :],
                                            gmax[:].unsqueeze(2).to_broadcast([P, NT, E]),
                                            ALU.subtract).then_inc(shifted_ready, 1)
                    if not last:
                        statistics(c + 1, i + u, 1 - u)
                    multiply(c, u, 0)
                    dve.wait_ge(exp_ready, c + 1)
                    nc.vector.tensor_reduce(gsum[:], expd[:], AX.X, ALU.add)
                    dve.drain()
                    nc.vector.reciprocal(grec[:], gsum[:])
                    dve.drain()
                    nc.vector.tensor_tensor(row[u][:, :, D:ROW], expd[:],
                                            grec[:].unsqueeze(2).to_broadcast([P, NT, E]),
                                            ALU.mult).then_inc(probs_ready, 1)
                    dve.drain()
                    nc.vector.tensor_tensor(biased[:], row[u][:, :, D:ROW],
                                            w.gate_b[:].unsqueeze(1).to_broadcast([P, NT, E]), ALU.add)
                    dve.drain()
                    for t in range(NT):
                        nc.vector.max(top[:, t, :], biased[:, t, :])
                    dve.drain()
                    for t in range(NT):
                        nc.vector.max_index(topi[:, t, :], top[:, t, :], biased[:, t, :])
                    dve.drain()
                    nc.vector.tensor_copy(topf[:], topi[:, :, 0:K])
                    dve.drain()
                    nc.vector.tensor_tensor(pick[:].rearrange("p t k e -> p (t k) e"),
                                            w.iota_expert[:].unsqueeze(1).to_broadcast([P, NT * K, E]),
                                            topf[:].rearrange("p t k -> p (t k)").unsqueeze(2).to_broadcast([P, NT * K, E]),
                                            ALU.is_equal)
                    dve.drain()
                    with nc.allow_low_precision("a sum of at most one 1"):
                        nc.vector.tensor_reduce(picked[:], pick[:].rearrange("p t k e -> p t e k"), AX.X,
                                                ALU.add).then_inc(picked_ready, 1)
                    multiply(c, u, 1)
                    multiply(c, u, 2)
                    dve.wait_ge(ranks_ready, c + 1)
                    nc.vector.tensor_tensor(prod[:], pick[:],
                                            p_gate[:, 1, :, :].unsqueeze(2).to_broadcast([P, NT, K, E]), ALU.mult)
                    nc.vector.tensor_reduce(newer[:], picked[:].rearrange("p t e -> p e t"), AX.X, ALU.add)
                    dve.drain()
                    nc.vector.tensor_reduce(rank[:], prod[:], AX.X, ALU.add)
                    nc.vector.tensor_tensor(earlier[:], earlier[:], newer[:], ALU.add)
                    for r in range(2):
                        if r == 1:
                            onehots(c)
                        dve.wait_ge(z_ready, 2 * c + r + 1)
                        nc.vector.scalar_tensor_tensor(x[u][:, 2 * r:2 * r + 2, :], p_z[:], 0.5,
                                                       x[u][:, 2 * r:2 * r + 2, :], ALU.mult,
                                                       ALU.add).then_inc(acc_ready, 1)

                loop(dve, chunk)
                dve.wait_ge(table_added, N)
                nc.vector.tensor_copy(table[:].rearrange("p a e -> p (a e)"), p_table[:, 0:2 * E])
                dve.drain()
                nc.vector.tensor_scalar(empty[:], table[:, 1, :], 0.0, w.dummy_row[:, 0:1], ALU.is_equal, ALU.mult)
                nc.vector.scalar_tensor_tensor(table[:, 0, :], table[:, 1, :], float(P), table[:, 0, :],
                                               ALU.mult, ALU.add)
                dve.drain()
                nc.vector.scalar_tensor_tensor(w.slot_token[:], table[:, 0, :], float(-P), empty[:],
                                               ALU.add, ALU.add)

            @block.tensor
            def _(pe):
                def turn(c, u, h):
                    pe.wait_ge(xn_ready, c + 1)
                    pe.wait_ge(xnT_ready, DC * c + h)
                    for t in range(NT):
                        last = nc.tensor.transpose(p_turn[:, t * P:(t + 1) * P], row[u][:, t, h * P:(h + 1) * P],
                                                   w.ident[:])
                    last.then_inc(turned, 1)

                pe.wait_ge(setup_done, 1)
                pe.wait_ge(shared_loaded, 16 * 5)
                nc.tensor.matmul(p_table[:], zero[:], w.ones_row[:], start=True, stop=True)
                for h in range(DC):
                    turn(0, 0, h)

                def chunk(c, i, u, last):
                    pe.wait_ge(xnT_ready, DC * c + DC)
                    pe.wait_ge(shifted_ready, c)
                    for t in range(NT):
                        for h in range(DC):
                            ins = nc.tensor.matmul(p_gate[:, 0, t, :], xnT[:, h, t * P:(t + 1) * P], w.gateT[:, h, :],
                                                   start=(h == 0), stop=(h == DC - 1))
                    ins.then_inc(logits_ready, 1)
                    for j in range(3):
                        n = (u + j) % RING
                        m = SJ[j]
                        pe.wait_ge(hidden_ready, 3 * c + j + 1)
                        for g, ws in enumerate((ws1T, ws3T)):
                            for h in range(DC):
                                ins = nc.tensor.matmul(p_up[n][g][0:m, :], ws[:, h, j * P:j * P + m], xnT[:, h, :],
                                                       start=(h == 0), stop=(h == DC - 1))
                        ins.then_inc(up_ready, 1)
                    if not last:
                        turn(c + 1, 1 - u, 0)
                    pe.wait_ge(picked_ready, c + 1)
                    for t in range(NT):
                        nc.tensor.matmul(p_gate[:, 1, t, :], w.before[:], picked[:, t, :], start=True, stop=False)
                        for s in range(t):
                            nc.tensor.matmul(p_gate[:, 1, t, :], w.ones[:], picked[:, s, :], start=False, stop=False)
                        ins = nc.tensor.matmul(p_gate[:, 1, t, :], w.ones[:], earlier[:], start=False, stop=True)
                    ins.then_inc(ranks_ready, 1)
                    for r in range(2):
                        pe.wait_ge(hidden_ready, 3 * c + 3 + RING)
                        pe.wait_ge(acc_ready, 2 * c + r)
                        for s in range(2):
                            t = 2 * r + s
                            for j in range(3):
                                m = SJ[j]
                                ins = nc.tensor.matmul(p_z[:, s, :], hidden[j][0:m, t * P:(t + 1) * P],
                                                       ws2T[0:m, j, :], start=(j == 0), stop=(j == 2))
                        ins.then_inc(z_ready, 1)
                        if r == 0 and not last:
                            turn(c + 1, 1 - u, 1)
                    pe.wait_ge(onehots_ready, c + 1)
                    for t in range(NT):
                        for k in range(K):
                            ins = nc.tensor.matmul(p_table[:, 0:2 * E], at_slot[:, t, k, :],
                                                   who[:, t, k, :, :].rearrange("p a e -> p (a e)"),
                                                   start=False, stop=True, skip_group_check=True)
                    ins.then_inc(table_added, 1)

                loop(pe, chunk)

def experts(nc, w, dram, acc, tag):
    WR = 4
    with ExitStack() as ctx:
        def sb(name, shape, dt=F32):
            return ctx.enter_context(nc.sbuf_tensor(f"{tag}_{name}", shape, dt))

        def ps(name, shape, dt=F32):
            return ctx.enter_context(nc.psum_tensor(f"{tag}_{name}", shape, dt))

        def sem(name):
            return ctx.enter_context(nc.semaphore(f"{tag}_{name}"))

        w13 = [sb(f"w13_{s}", [P, DC, SI]) for s in range(WR)]
        w2 = [sb(f"w2_{s}", [IH, 2, D]) for s in range(WR)]
        got = [sb(f"got{s}", [P, ROW]) for s in range(WR)]
        y = [sb(f"y{s}", [P, D]) for s in range(WR)]
        xT = [sb(f"xT{s}", [P, DC, CAP]) for s in range(2)]
        silu = [sb(f"silu{s}", [IH, 2, CAP]) for s in range(2)]
        hidden = [sb(f"hidden{s}", [IH, 2, CAP]) for s in range(2)]
        weight = sb("weight", [P, WR])

        p_turn = [ps(f"p_turn{s}", [P, DC, CAP]) for s in range(2)]
        p_up = [ps(f"p_up{s}", [P, 4, CAP]) for s in range(2)]
        p_y = [ps(f"p_y{s}", [P, D]) for s in range(2)]

        weights_loaded = [sem(f"weights_loaded{s}") for s in range(WR)]
        gathered = [sem(f"gathered{s}") for s in range(WR)]
        added = sem("added")
        y_free = sem("y_free")
        turned = sem("turned")
        xT_ready = sem("xT_ready")
        up_ready = sem("up_ready")
        silu_ready = sem("silu_ready")
        hidden_ready = sem("hidden_ready")
        y_ready = sem("y_ready")
        y_scaled = sem("y_scaled")

        with nc.Block() as block:
            @block.sync
            def _(sp):
                def load(e, q, s):
                    sp.dma_start(w13[s][:], dram.w13[e]).then_inc(weights_loaded[s], 16)
                    sp.dma_start(w2[s][:], dram.w2[e]).then_inc(weights_loaded[s], 16)

                for s in range(WR):
                    load(s, 0, s)
                with sp.Fori(1, E // WR) as q:
                    for s in range(WR):
                        sp.wait_ge(y_ready, WR * q + s - WR + 1)
                        load(WR * q + s, q, s)

            @block.gpsimd
            def _(pool):
                def gather(e, s):
                    nc.gpsimd.indirect_dma_start(
                        out=got[s][:], out_offset=None, in_=dram.rows,
                        in_offset=bass.IndirectOffsetOnAxis(ap=w.slot_token[:, e:e + 1].bitcast(U32), axis=0),
                    ).then_inc(gathered[s], 16)

                def add(e, s):
                    nc.gpsimd.indirect_dma_start(
                        out=acc, out_offset=bass.IndirectOffsetOnAxis(
                            ap=w.slot_token[:, e:e + 1].bitcast(U32), axis=0),
                        in_=y[s][:], in_offset=None, compute_op=ALU.add).then_inc(added, 16)

                pool.sem_inc(y_free, WR)
                for e in range(WR):
                    gather(e, e)
                for e in range(E):
                    pool.wait_ge(y_scaled, e + 1)
                    if e > 0:
                        pool.wait_ge(added, 16 * e)
                        pool.sem_inc(y_free, 1)
                    add(e, e % WR)
                    if e + WR < E:
                        gather(e + WR, e % WR)
                pool.wait_ge(added, 16 * E)

            @block.scalar
            def _(act):
                with act.Fori(0, E // 2) as i:
                    for s in range(2):
                        act.wait_ge(hidden_ready, 2 * i)
                        act.wait_ge(up_ready, 2 * i + s + 1)
                        nc.scalar.activation(silu[s][:], p_up[s][0:IH, 0:2, :], ACT.Silu).then_inc(silu_ready, 1)

            @block.vector
            def _(dve):
                def bring(e, q, s):
                    dve.wait_ge(turned, e + 1)
                    nc.vector.tensor_copy(xT[s % 2][:], p_turn[s % 2][:]).then_inc(xT_ready, 1)

                def multiply(e, q, s):
                    dve.wait_ge(silu_ready, e + 1)
                    nc.vector.tensor_tensor(hidden[s % 2][:], silu[s % 2][:], p_up[s % 2][0:IH, 2:4, :],
                                            ALU.mult).then_inc(hidden_ready, 1)

                def scale(e, q, s):
                    dve.wait_ge(y_ready, e + 1)
                    dve.wait_ge(y_free, e + 1)
                    nc.vector.tensor_scalar(y[s][:], p_y[s % 2][:], got[s][:, bass.ds(e + D, 1)], 0.5,
                                            ALU.mult, ALU.mult).then_inc(y_scaled, 1)

                pipeline(dve, bring, multiply, scale)

            @block.tensor
            def _(pe):
                def turn(e, q, s):
                    pe.wait_ge(gathered[s], 16 * q + 16)
                    for h in range(DC):
                        ins = nc.tensor.transpose(p_turn[s % 2][:, h, :], got[s][:, h * P:(h + 1) * P], w.ident[:])
                    ins.then_inc(turned, 1)

                def up(e, q, s):
                    pe.wait_ge(weights_loaded[s], 32 * q + 32)
                    pe.wait_ge(xT_ready, e + 1)
                    for g in range(4):
                        for h in range(DC):
                            ins = nc.tensor.matmul(p_up[s % 2][0:IH, g, :], w13[s][:, h, g * IH:(g + 1) * IH],
                                                   xT[s % 2][:, h, :], start=(h == 0), stop=(h == DC - 1))
                    ins.then_inc(up_ready, 1)

                def down(e, q, s):
                    pe.wait_ge(hidden_ready, e + 1)
                    for g in range(2):
                        ins = nc.tensor.matmul(p_y[s % 2][:], hidden[s % 2][:, g, :], w2[s][:, g, :],
                                               start=(g == 0), stop=(g == 1))
                    ins.then_inc(y_ready, 1)

                pipeline(pe, turn, up, down)



def pipeline(eng, first, second, third):
    first(0, 0, 0)
    first(1, 0, 1)
    second(0, 0, 0)
    with eng.Fori(0, E // 4 - 1) as q:
        for s in range(4):
            first(4 * q + s + 2, q + (s + 2) // 4, (s + 2) % 4)
            second(4 * q + s + 1, q + (s + 1) // 4, (s + 1) % 4)
            third(4 * q + s, q, s)
    last = E // 4 - 1
    for s in range(3):
        if s < 2:
            first(E - 2 + s, last, s + 2)
        second(E - 3 + s, last, s + 1)
        third(E - 4 + s, last, s)
    third(E - 1, last, 3)

HIGH, MIDDLE, LOW = range(3)
Q_SLOTS = [HIGH, HIGH, MIDDLE, HIGH, LOW, MIDDLE]
K_SLOTS = [HIGH, MIDDLE, HIGH, LOW, HIGH, MIDDLE]
SR = HD * len(Q_SLOTS)
QUADS = H // 4
HP = 32
PAGE = 64
SCALE = HD ** -0.5
SCORE_BANKS, MISC_BANKS, OUT_BANKS = 4, 2, 2

GROUPS = "ABC"
GROUP_ITEMS = {"A": 4, "B": 4, "C": 2}


def score_pieces(group, n):
    if group == "A":
        return [(n, 3, 0, 512)]
    if group == "B":
        return [(n, 2, 0, 384), (n, 0, 384, 128)]
    return [(2 * n, 1, 0, 256), (2 * n + 1, 1, 256, 256)]


PROJECT = [("XT", 0), ("XT", 1), ("Q", 0), ("QS", 0), ("Q", 1), ("QS", 1), ("SPLIT", 0), ("LAT", 0), ("SPLIT", 1),
           ("K", 0), ("KS", 0), ("K", 1), ("KS", 1), ("SPLIT", 2), ("V", 0), ("SPLIT", 3), ("V", 1)]
MAXIMA = [("S1", g, x) for g in range(QUADS) for x in GROUPS]
PROBS = [("S2", 0, "A"), ("S2", 0, "B"), ("PV", 0, "A"), ("S2", 0, "C"), ("PV", 0, "B"),
         ("S2", 1, "A"), ("PV", 0, "C"), ("S2", 1, "B"), ("PV", 1, "A"), ("OUT", 0), ("S2", 1, "C"), ("PV", 1, "B"),
         ("S2", 2, "A"), ("PV", 1, "C"), ("S2", 2, "B"), ("PV", 2, "A"), ("OUT", 1), ("S2", 2, "C"), ("PV", 2, "B"),
         ("S2", 3, "A"), ("PV", 2, "C"), ("S2", 3, "B"), ("PV", 3, "A"), ("OUT", 2), ("S2", 3, "C"), ("PV", 3, "B"),
         ("PV", 3, "C"), ("OUT", 3), ("AT", 0), ("AT", 1), ("WO", 0), ("WO", 1)]


def merged(main, side, start):
    out, side = [], list(side)
    for n, step in enumerate(main):
        out.append(step)
        if n >= start and side:
            out.append(side.pop(0))
    return out + side


FIRST_TURN = PROJECT + [("NORM",)] + MAXIMA + [("MAX",)]
TURN = PROJECT[:2] + merged(merged(PROBS[:14], PROJECT[2:], 0)
                            + PROBS[14:], [("NORM",)] + MAXIMA, 30) + [("MAX",)]
NEXT_TO_LAST_TURN = [s for s in TURN if s[0] != "NORM"]
LAST_TURN = list(PROBS)

MISC_STEPS = {"XT", "Q", "QS", "LAT", "K", "KS", "V", "OUT", "AT", "WO", "MAX"}


def count_misc(steps):
    return sum(s[0] in MISC_STEPS for s in steps)


def count_scores(steps):
    return sum(GROUP_ITEMS[s[2]] for s in steps if s[0] in ("S1", "S2"))


class Places:

    def __init__(self, banks, first, per_turn, turn):
        assert first % banks == 0 and per_turn % banks == 0
        self.banks, self.before, self.n = banks, first // banks + turn * (per_turn // banks), 0

    def next(self):
        bank, used = self.n % self.banks, self.before + self.n // self.banks
        self.n += 1
        return bank, used


def attention(nc, w, dram, src, dst, tag):
    with ExitStack() as ctx:
        def sb(name, shape, dt=F32):
            return ctx.enter_context(nc.sbuf_tensor(f"{tag}_{name}", shape, dt))

        def ps(name, shape, dt=F32):
            return ctx.enter_context(nc.psum_tensor(f"{tag}_{name}", shape, dt))

        def sem(name):
            return ctx.enter_context(nc.semaphore(f"{tag}_{name}"))

        wq, wq_swap = sb("wq", [P, DC, D]), sb("wq_swap", [P, DC, D])
        w_down = sb("w_down", [P, DC, P])
        wk, wk_swap, wv = sb("wk", [P, D]), sb("wk_swap", [P, D]), sb("wv", [P, D])
        wo = sb("wo", [P, DC, D])
        cos, sin = sb("cos", [P, T]), sb("sin", [P, T])
        mask_f = sb("mask_f", [P, 2 * P])
        mask = sb("mask", [P, 2 * P], BF16)
        far = sb("far", [P, PAGE], BF16)
        ident16 = sb("ident16", [P, P], BF16)

        x = sb("x", [P, NT, D])
        residual = sb("residual", [P, NT, D])
        stats, mv = sb("stats", [P, NT, 6]), sb("mv", [P, NT, 2])
        rstd, shift = sb("rstd", [P, NT]), sb("shift", [P, NT])
        xnT = sb("xnT", [P, DC, T])
        latT = sb("latT", [P, T])
        by_sin = sb("by_sin", [P, T])
        qk = [sb(f"qk{r}", [P, T]) for r in range(4)]
        parts = [sb(f"parts{r}", [P, 3, T], BF16) for r in range(4)]
        qs = [sb(f"qs{u}", [P, H, T], BF16) for u in range(2)]
        ks = [sb(f"ks{u}", [P, H, T], BF16) for u in range(2)]
        v = [sb(f"v{u}", [P, NT, H, HP]) for u in range(2)]
        probs = [sb(f"probs{n}", [P, T]) for n in range(10)]
        outT = [sb(f"outT{n}", [P, T]) for n in range(OUT_BANKS)]
        rsum = sb("rsum", [P, NT, 4])
        attn = sb("attn", [P, NT, D])
        attnT = xnT
        smax = sb("smax", [P, NT, H])
        smax_rest = sb("smax_rest", [P, NT, H])
        smax_parts = sb("smax_parts", [P, NT, P], BF16)
        smaxT = sb("smaxT", [3 * H, T], BF16)

        p_score = [ps(f"p_score{n}", [P, T]) for n in range(SCORE_BANKS)]
        p_out = [ps(f"p_out{n}", [P, T]) for n in range(OUT_BANKS)]
        p_misc = [ps(f"p_misc{n}", [P, T]) for n in range(MISC_BANKS)]

        setup_loaded, setup_done = sem("setup_loaded"), sem("setup_done")
        x_loaded = sem("x_loaded")
        residual_loaded = sem("residual_loaded")
        stats_ready, scales_ready, xn_ready = sem("stats_ready"), sem("scales_ready"), sem("xn_ready")
        rope_ready, high_ready, rest_ready = sem("rope_ready"), sem("high_ready"), sem("rest_ready")
        middle_ready, low_ready = sem("middle_ready"), sem("low_ready")
        parts_stored, stack_loaded = sem("parts_stored"), sem("stack_loaded")
        misc_ready = [sem(f"misc_ready{n}") for n in range(MISC_BANKS)]
        misc_free = [sem(f"misc_free{n}") for n in range(MISC_BANKS)]
        score_ready = [sem(f"score_ready{n}") for n in range(SCORE_BANKS)]
        score_free = [sem(f"score_free{n}") for n in range(SCORE_BANKS)]
        smax_parts_ready = sem("smax_parts_ready")
        smax_stored, smax_loaded = sem("smax_stored"), sem("smax_loaded")
        quad_done, outT_ready = sem("quad_done"), sem("outT_ready")
        result_stored = sem("result_stored")

        def misc_places(b):
            return Places(MISC_BANKS, count_misc(FIRST_TURN), count_misc(TURN), b)

        def score_places(b):
            return Places(SCORE_BANKS, count_scores(FIRST_TURN), count_scores(TURN), b)

        def turns(eng, turn):
            turn(None, 1, 0, FIRST_TURN, Places(MISC_BANKS, 0, 0, 0), Places(SCORE_BANKS, 0, 0, 0))
            with eng.Fori(0, B // 2 - 1) as i:
                for u in range(2):
                    b = 2 * i + u
                    turn(b, u, b + 1, TURN, misc_places(b), score_places(b))
            turn(B - 2, 0, B - 1, NEXT_TO_LAST_TURN, misc_places(B - 2), score_places(B - 2))
            turn(B - 1, 1, None, LAST_TURN, misc_places(B - 1), score_places(B - 1))

        with nc.Block() as block:
            @block.sync
            def _(sp):
                for to, fro in ((wq[:], dram.wq), (wq_swap[:], dram.wq_swap), (w_down[:], dram.w_down),
                                (wk[:], dram.wk), (wk_swap[:], dram.wk_swap), (wv[:], dram.wv), (wo[:], dram.wo),
                                (cos[:], dram.cos), (sin[:], dram.sin), (mask_f[:], dram.mask)):
                    sp.dma_start(to, fro).then_inc(setup_loaded, 16)
                sp.dma_start(x[:], src[0]).then_inc(x_loaded, 16)

                def store_parts(r, n, u):
                    sp.wait_ge(low_ready, 4 * n + r + 1)
                    sp.dma_start(dram.parts[u, r // 2, :, (r % 2) * P:(r % 2 + 1) * P, :].rearrange("s p t -> p s t"),
                                 parts[r][:]).then_inc(parts_stored, 16)

                def stack(r, n, u):
                    sp.wait_ge(parts_stored, 64 * n + 16 * r + 16)
                    to, slots = ((qs, Q_SLOTS), (ks, K_SLOTS))[r // 2]
                    for s, part in enumerate(slots):
                        sp.dma_start(to[u][s * HD:(s + 1) * HD, :, :],
                                     dram.parts[u, r // 2, part, :, :].rearrange("(h d) t -> d h t", d=HD)
                                     ).then_inc(stack_loaded, 16)

                def turn(b, u, n, steps, misc, scores):
                    if b is not None:
                        sp.wait_ge(result_stored, 16 * b)
                        sp.dma_start(residual[:], src[b]).then_inc(residual_loaded, 16)
                    for step in steps:
                        if step[0] in MISC_STEPS:
                            m, used = misc.next()
                        if step == ("XT", 1) and ("NORM",) in steps:
                            sp.wait_ge(misc_free[m], used + 1)
                            sp.dma_start(x[:], src[n + 1]).then_inc(x_loaded, 16)
                        if step[0] == "SPLIT":
                            r = step[1]
                            store_parts(r, n, 1 - u)
                            if r % 2:
                                stack(r, n, 1 - u)
                        elif step[0] == "MAX":
                            sp.wait_ge(misc_free[m], used + 1)
                            sp.dma_start(dram.smax[1 - u], smaxT[:]).then_inc(smax_stored, 16)
                            sp.wait_ge(smax_stored, 16 * n + 16)
                            sp.dma_start(qs[1 - u][SR:SR + 3, :, :],
                                         dram.smax[1 - u].rearrange("(s h) t -> s h t", h=H)
                                         ).then_inc(smax_loaded, 16)
                        elif step == ("WO", 1):
                            sp.wait_ge(misc_free[m], used + 1)
                            sp.dma_start(dst[b], residual[:]).then_inc(result_stored, 16)

                turns(sp, turn)
                sp.wait_ge(result_stored, 16 * B)

            @block.gpsimd
            def _(pool):
                def scales(n):
                    pool.wait_ge(xn_ready, n)
                    pool.wait_ge(stats_ready, n + 1)
                    token_scales(nc, pool, mv, rstd, shift, w).then_inc(scales_ready, 1)

                def turn(b, u, n, steps, misc, scores):
                    for step in steps:
                        if step[0] == "SPLIT":
                            r = step[1]
                            pool.wait_ge(middle_ready, 4 * n + r + 1)
                            nc.gpsimd.tensor_tensor(parts[r][:, LOW, :], qk[r][:], parts[r][:, MIDDLE, :],
                                                    ALU.subtract).then_inc(low_ready, 1)
                        elif step[0] == "NORM":
                            scales(n + 1)

                scales(0)
                turns(pool, turn)

            @block.scalar
            def _(act):
                def normalise(n):
                    act.wait_ge(scales_ready, n + 1)
                    token_normalise(nc, x, rstd, shift, x).then_inc(xn_ready, 1)

                def turn(b, u, n, steps, misc, scores):
                    def bank():
                        m, used = misc.next()
                        return m, used + 1

                    for step in steps:
                        kind = step[0]
                        if kind == "S1":
                            for _ in range(GROUP_ITEMS[step[2]]):
                                scores.next()
                        elif kind == "S2":
                            for k in range(GROUP_ITEMS[step[2]]):
                                s, used = scores.next()
                                act.wait_ge(score_ready[s], used + 1)
                                to = probs[{"A": 0, "B": 4, "C": 8}[step[2]] + k]
                                nc.scalar.activation(to[:], p_score[s][:], ACT.Exp, scale=SCALE
                                                     ).then_inc(score_free[s], 1)
                        elif kind == "PV" and step[2] == "C":
                            act.wait_ge(quad_done, QUADS * b + step[1] + 1)
                            nc.scalar.copy(outT[step[1] % OUT_BANKS][:], p_out[step[1] % OUT_BANKS][:]
                                           ).then_inc(outT_ready, 1)
                        elif kind == "XT":
                            m, use = bank()
                            act.wait_ge(misc_ready[m], use)
                            nc.scalar.copy(xnT[:, step[1], :], p_misc[m][:]).then_inc(misc_free[m], 1)
                        elif kind == "LAT":
                            m, use = bank()
                            act.wait_ge(misc_ready[m], use)
                            nc.scalar.copy(latT[:], p_misc[m][:]).then_inc(misc_free[m], 1)
                        elif kind == "V":
                            m, use = bank()
                            act.wait_ge(misc_ready[m], use)
                            for s in range(2):
                                ins = nc.scalar.copy(v[1 - u][:, 2 * step[1] + s, :, 0:HD],
                                                     p_misc[m][:, s * D:(s + 1) * D].rearrange("p (h d) -> p h d", d=HD))
                            ins.then_inc(misc_free[m], 1)
                        elif kind == "AT":
                            m, use = bank()
                            act.wait_ge(misc_ready[m], use)
                            nc.scalar.copy(attnT[:, step[1], :], p_misc[m][:]).then_inc(misc_free[m], 1)
                        elif kind == "MAX":
                            m, use = bank()
                            act.wait_ge(smax_loaded, 16 * n)
                            act.wait_ge(misc_ready[m], use)
                            nc.scalar.copy(smaxT[:], p_misc[m][0:3 * H, 0:T // 2].bitcast(BF16)
                                           ).then_inc(misc_free[m], 1)
                        elif kind in MISC_STEPS:
                            misc.next()
                        if kind in ("QS", "KS"):
                            r = step[1] + (2 if kind == "KS" else 0)
                            act.wait_ge(parts_stored, 64 * n)
                            act.wait_ge(rope_ready, 4 * n + r + 1)
                            nc.scalar.copy(parts[r][:, HIGH, :], qk[r][:]).then_inc(high_ready, 1)
                        elif kind == "SPLIT":
                            r = step[1]
                            act.wait_ge(rest_ready, 4 * n + r + 1)
                            nc.scalar.copy(parts[r][:, MIDDLE, :], qk[r][:]).then_inc(middle_ready, 1)
                        elif kind == "NORM":
                            normalise(n + 1)

                normalise(0)
                act.wait_ge(setup_done, 1)
                turns(act, turn)

            @block.vector
            def _(dve):
                dve.wait_ge(setup_loaded, 160)
                nc.vector.tensor_copy(mask[:], mask_f[:])
                nc.vector.tensor_copy(ident16[:], w.ident[:])
                nc.vector.memset(far[:], 0.0)
                nc.vector.memset(smax_parts[:], 0.0)
                for u in range(2):
                    nc.vector.memset(v[u][:], 0.0)
                    nc.vector.memset(ks[u][SR:SR + 3, :, :], 1.0)
                dve.drain()
                nc.vector.memset(far[0:1, :], -2.0 ** 100)
                for u in range(2):
                    nc.vector.memset(v[u][:, :, :, HD:HD + 1], 1.0)
                dve.drain()
                dve.sem_inc(setup_done, 1)

                def statistics(n):
                    dve.wait_ge(x_loaded, 16 * n + 16)
                    dve.wait_ge(scales_ready, n)
                    token_stats(nc, dve, x, stats, mv).then_inc(stats_ready, 1)

                def turn(b, u, n, steps, misc, scores):
                    for step in steps:
                        kind = step[0]
                        m, use = misc.next() if kind in MISC_STEPS else (None, None)
                        if kind == "S2":
                            for _ in range(GROUP_ITEMS[step[2]]):
                                scores.next()
                        elif kind == "S1":
                            for k in range(GROUP_ITEMS[step[2]]):
                                s, used = scores.next()
                                dve.wait_ge(score_ready[s], used + 1)
                                h0 = 4 * step[1]
                                if step[2] == "C":
                                    ins = nc.vector.tensor_reduce(
                                        smax[:, 1, h0 + 2 * k:h0 + 2 * k + 2],
                                        p_score[s][:].rearrange("p (h t) -> p h t", h=2), AX.X, ALU.max)
                                else:
                                    for h, t, at, length in score_pieces(step[2], k):
                                        ins = nc.vector.tensor_reduce(smax[:, t, h0 + h:h0 + h + 1],
                                                                      p_score[s][:, at:at + length], AX.X, ALU.max)
                                ins.then_inc(score_free[s], 1)
                        elif kind in ("Q", "K"):
                            r = step[1] + (2 if kind == "K" else 0)
                            dve.wait_ge(low_ready, 4 * n)
                            dve.wait_ge(misc_ready[m], use + 1)
                            nc.vector.tensor_tensor(qk[r][:], p_misc[m][:], cos[:], ALU.mult
                                                    ).then_inc(misc_free[m], 1)
                        elif kind in ("QS", "KS"):
                            r = step[1] + (2 if kind == "KS" else 0)
                            dve.wait_ge(misc_ready[m], use + 1)
                            nc.vector.tensor_tensor(by_sin[:], p_misc[m][:], sin[:], ALU.mult
                                                    ).then_inc(misc_free[m], 1)
                            dve.drain()
                            nc.vector.tensor_tensor(qk[r][:], qk[r][:], by_sin[:], ALU.add
                                                    ).then_inc(rope_ready, 1)
                            dve.drain()
                        elif kind == "SPLIT":
                            r = step[1]
                            dve.wait_ge(high_ready, 4 * n + r + 1)
                            nc.vector.tensor_tensor(qk[r][:], qk[r][:], parts[r][:, HIGH, :],
                                                    ALU.subtract).then_inc(rest_ready, 1)
                        elif kind == "NORM":
                            statistics(n + 1)
                        elif kind == "MAX":
                            dve.drain()
                            nc.vector.tensor_scalar(smax[:], smax[:], -1.0, None, ALU.mult)
                            dve.drain()
                            nc.vector.tensor_copy(smax_parts[:, :, 0:H], smax[:])
                            dve.drain()
                            nc.vector.tensor_tensor(smax_rest[:], smax[:], smax_parts[:, :, 0:H], ALU.subtract)
                            dve.drain()
                            nc.vector.tensor_copy(smax_parts[:, :, H:2 * H], smax_rest[:])
                            dve.drain()
                            nc.vector.tensor_tensor(smax_parts[:, :, 2 * H:3 * H], smax_rest[:],
                                                    smax_parts[:, :, H:2 * H], ALU.subtract
                                                    ).then_inc(smax_parts_ready, 1)
                        elif kind == "OUT":
                            g = step[1]
                            out = p_misc[m][:].rearrange("p (t h c) -> p t h c", t=NT, h=4)
                            dve.wait_ge(misc_ready[m], use + 1)
                            nc.vector.reciprocal(rsum[:], out[:, :, :, HD])
                            dve.drain()
                            nc.vector.tensor_tensor(
                                attn[:, :, g * 4 * HD:(g + 1) * 4 * HD].rearrange("p t (h d) -> p t h d", d=HD),
                                out[:, :, :, 0:HD], rsum[:].unsqueeze(3).to_broadcast([P, NT, 4, HD]),
                                ALU.mult).then_inc(misc_free[m], 1)
                            dve.drain()
                        elif kind == "WO":
                            r = step[1]
                            dve.wait_ge(residual_loaded, 16 * b + 16)
                            dve.wait_ge(misc_ready[m], use + 1)
                            nc.vector.tensor_tensor(residual[:, 2 * r:2 * r + 2, :],
                                                    p_misc[m][:].rearrange("p (t d) -> p t d", t=2),
                                                    residual[:, 2 * r:2 * r + 2, :], ALU.add
                                                    ).then_inc(misc_free[m], 1)

                statistics(0)
                turns(dve, turn)

            @block.tensor
            def _(pe):
                pe.wait_ge(setup_done, 1)

                def turn(b, u, n, steps, misc, scores):
                    def take_misc():
                        m, used = misc.next()
                        pe.wait_ge(misc_free[m], used)
                        freed[step] = m, used + 1
                        return m

                    def wait_read(of):
                        pe.wait_ge(misc_free[freed[of][0]], freed[of][1])

                    def take_score():
                        s, used = scores.next()
                        pe.wait_ge(score_free[s], used)
                        return s

                    freed = {}
                    for step in steps:
                        kind = step[0]
                        if kind == "S1":
                            g, group = step[1:]
                            if (g, group) == (0, "A"):
                                pe.wait_ge(stack_loaded, 192 * n + 192)
                            for k in range(GROUP_ITEMS[group]):
                                s = take_score()
                                for h, t, at, length in score_pieces(group, k):
                                    head = 4 * g + h
                                    nc.tensor.matmul(p_score[s][:, at:at + length],
                                                     qs[1 - u][0:SR, head, t * P:(t + 1) * P],
                                                     ks[1 - u][0:SR, head, 0:length], start=True, stop=True)
                                    ins = nc.tensor.matmul(p_score[s][:, at + length - PAGE:at + length],
                                                           mask[:, 0:P], far[:], start=False, stop=True,
                                                           skip_group_check=True)
                                ins.then_inc(score_ready[s], 1)
                        elif kind == "S2":
                            g, group = step[1:]
                            if (g, group) == (0, "A"):
                                pe.wait_ge(smax_loaded, 16 * b + 16)
                            for k in range(GROUP_ITEMS[group]):
                                s = take_score()
                                for h, back, at, length in score_pieces(group, k):
                                    head, t = 4 * g + h, NT - 1 - back
                                    nc.tensor.matmul(p_score[s][:, at:at + length],
                                                     ks[u][0:SR + 3, head, t * P:(t + 1) * P],
                                                     qs[u][0:SR + 3, head, t * P:T], start=True, stop=True)
                                    ins = nc.tensor.matmul(p_score[s][:, at:at + PAGE],
                                                           mask[:, P:2 * P], far[:], start=False, stop=True,
                                                           skip_group_check=True)
                                ins.then_inc(score_ready[s], 1)
                            freed[step[1:]] = s, scores.before + (scores.n - 1) // SCORE_BANKS + 1
                        elif kind == "PV":
                            g, group = step[1:]
                            pe.wait_ge(score_free[freed[step[1:]][0]], freed[step[1:]][1])
                            for piece in range(2 if group == "B" else 1):
                                for h in range(4):
                                    k = {"A": h, "B": 4 + h, "C": 8 + h // 2}[group]
                                    of = score_pieces(group, h // 2 if group == "C" else h)
                                    _, back, at, length = of[h % 2 if group == "C" else piece]
                                    t = NT - 1 - back
                                    ins = nc.tensor.matmul(p_out[g % OUT_BANKS][h * HP:(h + 1) * HP, t * P:T],
                                                           v[u][:, t, 4 * g + h, :], probs[k][:, at:at + length],
                                                           start=(group == "A"), stop=True,
                                                           skip_group_check=True)
                            if group == "C":
                                ins.then_inc(quad_done, 1)
                        elif kind == "OUT":
                            g = step[1]
                            pe.wait_ge(outT_ready, QUADS * b + g + 1)
                            m = take_misc()
                            for t in range(NT):
                                ins = nc.tensor.transpose(p_misc[m][:, t * P:(t + 1) * P],
                                                          outT[g % OUT_BANKS][:, t * P:(t + 1) * P], w.ident[:])
                            ins.then_inc(misc_ready[m], 1)
                        elif kind == "AT":
                            m = take_misc()
                            if step[1] == 0:
                                wait_read(("OUT", 3))
                            for t in range(NT):
                                ins = nc.tensor.transpose(p_misc[m][:, t * P:(t + 1) * P],
                                                          attn[:, t, step[1] * P:(step[1] + 1) * P], w.ident[:])
                            ins.then_inc(misc_ready[m], 1)
                        elif kind == "WO":
                            m = take_misc()
                            if step[1] == 0:
                                wait_read(("AT", 1))
                            for s in range(2):
                                t = 2 * step[1] + s
                                for h in range(DC):
                                    ins = nc.tensor.matmul(p_misc[m][:, s * D:(s + 1) * D],
                                                           attnT[:, h, t * P:(t + 1) * P], wo[:, h, :],
                                                           start=(h == 0), stop=(h == DC - 1))
                            ins.then_inc(misc_ready[m], 1)
                        elif kind == "MAX":
                            m = take_misc()
                            pe.wait_ge(smax_parts_ready, n + 1)
                            for t in range(NT):
                                ins = nc.tensor.transpose(p_misc[m][:, t * P // 2:(t + 1) * P // 2].bitcast(BF16),
                                                          smax_parts[:, t, :], ident16[:])
                            ins.then_inc(misc_ready[m], 1)
                        elif kind == "XT":
                            m = take_misc()
                            pe.wait_ge(xn_ready, n + 1)
                            for t in range(NT):
                                ins = nc.tensor.transpose(p_misc[m][:, t * P:(t + 1) * P],
                                                          x[:, t, step[1] * P:(step[1] + 1) * P], w.ident[:])
                            ins.then_inc(misc_ready[m], 1)
                        elif kind in ("Q", "QS", "LAT"):
                            weights = {"Q": wq, "QS": wq_swap, "LAT": w_down}[kind]
                            m = take_misc()
                            if step == ("Q", 0):
                                wait_read(("XT", 1))
                            for h in range(DC):
                                ins = nc.tensor.matmul(p_misc[m][:], weights[:, h, step[1] * P:(step[1] + 1) * P],
                                                       xnT[:, h, :], start=(h == 0), stop=(h == DC - 1))
                            ins.then_inc(misc_ready[m], 1)
                        elif kind in ("K", "KS"):
                            weights = {"K": wk, "KS": wk_swap}[kind]
                            m = take_misc()
                            if step == ("K", 0):
                                wait_read(("LAT", 0))
                            ins = nc.tensor.matmul(p_misc[m][:], weights[:, step[1] * P:(step[1] + 1) * P], latT[:],
                                                   start=True, stop=True)
                            ins.then_inc(misc_ready[m], 1)
                        elif kind == "V":
                            m = take_misc()
                            for s in range(2):
                                t = 2 * step[1] + s
                                ins = nc.tensor.matmul(p_misc[m][:, s * D:(s + 1) * D], latT[:, t * P:(t + 1) * P],
                                                       wv[:], start=True, stop=True)
                            ins.then_inc(misc_ready[m], 1)

                turns(pe, turn)


class Resident:
    pass


def load_resident(nc, ctx, dram):
    def sb(name, shape, dt=F32):
        return ctx.enter_context(nc.sbuf_tensor(name, shape, dt))

    w = Resident()
    w.gateT = sb("gateT", [P, DC, E])
    w.gate_b = sb("gate_b", [P, E])
    w.ident = sb("ident", [P, P])
    w.iota_slot = sb("iota_slot", [P, CAP], BF16)
    iota_slot_f = sb("iota_slot_f", [P, CAP])
    w.iota_expert = sb("iota_expert", [P, E])
    w.small = sb("small", [P, 8])
    w.lane = w.small[:, 0:1]
    w.dummy_row = w.small[:, 1:2]
    w.first_tiles = w.small[:, 4:8]
    w.minus_one = sb("minus_one", [P, NT])
    w.minus_half = sb("minus_half", [P, NT])
    w.eps = sb("eps", [P, NT])
    w.tiles_per_chunk = sb("tiles_per_chunk", [P, NT])
    w.before = sb("before", [P, P], BF16)
    w.ones = sb("ones", [P, P], BF16)
    w.ones_row = sb("ones_row", [P, T], BF16)
    w.slot_token = sb("slot_token", [P, E], I32)
    before_f = sb("before_f", [P, P])
    loaded = ctx.enter_context(nc.semaphore("resident_loaded"))
    wrote = ctx.enter_context(nc.semaphore("dummy_rows_written"))
    zeroed = ctx.enter_context(nc.semaphore("zeroed"))
    blank = sb("blank", [P, ROW])

    with nc.Block() as block:
        @block.sync
        def _(sp):
            n = 0
            for dst, src in ((w.gateT, dram.gateT), (w.gate_b, dram.gate_b), (w.ident, dram.ident), (w.small, dram.small),
                             (iota_slot_f, dram.iota_slot), (w.iota_expert, dram.iota_expert), (before_f, dram.before)):
                sp.dma_start(dst[:], src).then_inc(loaded, 16)
                n += 16
            sp.wait_ge(zeroed, 1)
            sp.dma_start(dram.rows[DUMMY:DUMMY + P, :], blank[:]).then_inc(wrote, 16)
            for a in dram.accs:
                sp.dma_start(a[DUMMY:DUMMY + P, :], blank[:, 0:D]).then_inc(wrote, 16)
            sp.wait_ge(loaded, n)
            sp.wait_ge(wrote, 16 * (1 + len(dram.accs)))

        @block.vector
        def _(dve):
            nc.vector.memset(blank[:], 0.0)
            nc.vector.memset(w.ones[:], 1.0)
            nc.vector.memset(w.minus_half[:], -0.5)
            nc.vector.memset(w.minus_one[:], -1.0)
            nc.vector.memset(w.eps[:], EPS)
            nc.vector.memset(w.tiles_per_chunk[:], float(NT))
            nc.vector.memset(w.ones_row[:], 1.0)
            dve.drain()
            dve.sem_inc(zeroed, 1)
            dve.wait_ge(loaded, 16 * 7)
            nc.vector.tensor_copy(w.before[:], before_f[:])
            nc.vector.tensor_copy(w.iota_slot[:], iota_slot_f[:])
    return w


class Dram:
    pass


def program(nc, dram):
    with ExitStack() as ctx:
        w = load_resident(nc, ctx, dram)
        route_and_share(nc, w, dram, dram.x_chunks, dram.acc1_chunks, "f1")
        experts(nc, w, dram, dram.accs[0], "e1")
        attention(nc, w, dram, dram.acc1_chunks, dram.mid, "a")
        route_and_share(nc, w, dram, dram.mid, dram.out_chunks, "f2")
        experts(nc, w, dram, dram.out_rows, "e2")


def kernel(**inputs):
    import numpy as np
    import concourse.bacc as bacc
    from concourse.bass_utils import run_bass_kernel_spmd

    nc = bacc.Bacc("TRN2", target_bir_lowering=False, num_devices=1)
    arrays = {}

    def put(name, a):
        a = np.ascontiguousarray(a)
        arrays[name] = a
        return nc.dram_tensor(name, a.shape, mybir.dt.from_np(a.dtype), kind="ExternalInput").ap()

    def halves(a):
        return a.reshape(2, P, -1).transpose(1, 0, 2)

    g = {k.removeprefix("L0_"): np.asarray(v) for k, v in inputs.items()}
    dram = Dram()
    chunked = "(c t p) d -> c p t d"
    dram.x_chunks = put("x_in", g["attn_x"].reshape(TOK, D)).rearrange(chunked, p=P, t=NT)
    dram.gateT = put("gateT_in", halves(g["ffn_gate_w"].T))
    dram.gate_b = put("gate_b_in", np.broadcast_to(g["ffn_gate_b"], (P, E)))
    dram.ws1T = put("ws1T_in", halves(g["ffn_ws1"].T))
    dram.ws3T = put("ws3T_in", halves(g["ffn_ws3"].T))
    dram.ws2T = put("ws2T_in", g["ffn_ws2"].T)
    w13 = np.concatenate([g["ffn_w1"], g["ffn_w3"]], axis=1)
    dram.w13 = put("w13_in", w13.transpose(0, 2, 1).reshape(E, DC, P, SI).transpose(0, 2, 1, 3))
    dram.w2 = put("w2_in", g["ffn_w2"].transpose(0, 2, 1).reshape(E, 2, IH, D).transpose(0, 2, 1, 3))
    lanes = np.arange(P, dtype=np.float32)
    dram.ident = put("ident_in", np.eye(P, dtype=np.float32))
    dram.before = put("before_in", np.triu(np.ones((P, P), np.float32), 1))
    dram.iota_slot = put("iota_slot_in", np.broadcast_to(lanes, (P, CAP)))
    dram.iota_expert = put("iota_expert_in", np.broadcast_to(lanes[:E], (P, E)))
    small = np.zeros((P, 8), np.float32)
    small[:, 0] = lanes
    small[:, 1] = DUMMY + P + lanes
    small[:, 4:8] = 1 + np.arange(NT) - NT
    dram.small = put("small_in", small)

    def scratch(name, shape, dt=F32):
        return nc.dram_tensor(name, shape, dt, kind="Internal").ap()

    dram.rows = scratch("rows", [TOK + P, ROW])
    dram.accs = [scratch(f"acc{n}", [TOK + P, D]) for n in range(1)]
    dram.rows_chunks = dram.rows[0:TOK, :].rearrange(chunked, p=P, t=NT)
    dram.acc1_chunks = dram.accs[0][0:TOK, :].rearrange(chunked, p=P, t=NT)
    dram.mid = scratch("mid", [TOK, D]).rearrange(chunked, p=P, t=NT)
    swap = np.arange(D).reshape(-1, 2)[:, ::-1].reshape(-1)
    dram.wq, dram.wq_swap = put("wq_in", halves(g["attn_wq"])), put("wq_swap_in", halves(g["attn_wq"][:, swap]))
    dram.w_down = put("w_down_in", halves(g["attn_w_down"]))
    dram.wk, dram.wk_swap = put("wk_in", g["attn_wk_up"]), put("wk_swap_in", g["attn_wk_up"][:, swap])
    dram.wv = put("wv_in", g["attn_wv_up"])
    dram.wo = put("wo_in", halves(g["attn_wo"]))
    inv = 1.0 / 10000.0 ** (np.arange(0, HD, 2, dtype=np.float32) / HD)
    angle = np.outer(np.arange(T, dtype=np.float32), inv)
    dram.cos = put("cos_in", np.tile(np.repeat(np.cos(angle).T, 2, axis=0), (P // HD, 1)).astype(np.float32))
    signed = np.stack([-np.sin(angle).T, np.sin(angle).T], axis=1).reshape(HD, T)
    dram.sin = put("sin_in", np.tile(signed, (P // HD, 1)).astype(np.float32))
    mask = np.zeros((P, 2 * P), np.float32)
    mask[0, 0:PAGE] = 1
    mask[0, P + PAGE:] = 1
    dram.mask = put("mask_in", mask)
    dram.parts = scratch("parts", [2, 2, 3, D, T], BF16)
    dram.smax = scratch("smax", [2, 3 * H, T], BF16)
    out = nc.dram_tensor("out", (TOK + P, D), F32, kind="ExternalOutput").ap()
    dram.out_rows = out
    dram.out_chunks = out[0:TOK, :].rearrange(chunked, p=P, t=NT)
    dram.accs.append(dram.out_rows)
    program(nc, dram)
    got = run_bass_kernel_spmd(nc, [arrays], core_ids=[0])
    return got.results[0]["out"][0:TOK].reshape(B, T, D)
```

```python
import concourse.bass as bass
from concourse import mybir
from contextlib import ExitStack

F32 = mybir.dt.float32
BF16 = mybir.dt.bfloat16
I32 = mybir.dt.int32
U32 = mybir.dt.uint32
ALU = mybir.AluOpType
ACT = mybir.ActivationFunctionType
AX = mybir.AxisListType

P = 128
B, T, D = 16, 512, 256
TOK = B * T
NT = T // P
DC = D // P
E, K, CAP = 64, 6, 128
I = 176
IH = I // 2
SI = 2 * I
SJ = [128, 128, SI - 256]
ROW = D + E
DUMMY = TOK
H, HD = 16, 16
EPS = 1e-5
RING = 2


def token_stats(nc, dve, x, stats, mv):
    for t in range(NT):
        nc.vector.bn_stats(stats[:, t, :], x[:, t, :])
    dve.drain()
    for t in range(NT):
        last = nc.vector.bn_aggr(mv[:, t, :], stats[:, t, :])
    return last


def token_scales(nc, pool, mv, rstd, shift, w):
    nc.gpsimd.tensor_tensor(rstd[:], mv[:, :, 1], w.eps[:], ALU.add)
    nc.gpsimd.tensor_tensor(shift[:], mv[:, :, 0], w.minus_one[:], ALU.mult)
    pool.drain()
    nc.gpsimd.tensor_tensor(rstd[:], rstd[:], w.minus_half[:], ALU.pow)
    pool.drain()
    return nc.gpsimd.tensor_tensor(shift[:], shift[:], rstd[:], ALU.mult)


def token_normalise(nc, x, rstd, shift, xn):
    for t in range(NT):
        last = nc.scalar.activation(xn[:, t, 0:D], x[:, t, :], ACT.Identity, bias=shift[:, t:t + 1],
                                    scale=rstd[:, t:t + 1])
    return last


def wait_count(eng, semaphore, count):
    if not isinstance(count, int) or count > 0:
        eng.wait_ge(semaphore, count)


def route_and_share(nc, w, dram, src, acc, tag):
    N = B
    with ExitStack() as ctx:
        def sb(name, shape, dt=F32):
            return ctx.enter_context(nc.sbuf_tensor(f"{tag}_{name}", shape, dt))

        def ps(name, shape, dt=F32):
            return ctx.enter_context(nc.psum_tensor(f"{tag}_{name}", shape, dt))

        def sem(name):
            return ctx.enter_context(nc.semaphore(f"{tag}_{name}"))

        ws1T, ws3T = sb("ws1T", [P, DC, SI]), sb("ws3T", [P, DC, SI])
        ws2T = sb("ws2T", [P, 3, D])
        x = [sb(f"x{u}", [P, NT, D]) for u in range(2)]
        row = [sb(f"row{u}", [P, NT, ROW]) for u in range(2)]
        stats = sb("stats", [P, NT, 6])
        mv = sb("mv", [P, NT, 2])
        rstd = sb("rstd", [P, NT])
        shift = sb("shift", [P, NT])
        xnT = sb("xnT", [P, DC, T])
        gmax = sb("gmax", [P, NT])
        shifted = sb("shifted", [P, NT, E])
        expd = sb("expd", [P, NT, E])
        gsum = sb("gsum", [P, NT])
        grec = sb("grec", [P, NT])
        biased = sb("biased", [P, NT, E])
        top = sb("top", [P, NT, 8])
        topi = sb("topi", [P, NT, 8], U32)
        topf = sb("topf", [P, NT, K])
        pick = sb("pick", [P, NT, K, E], BF16)
        picked = sb("picked", [P, NT, E], BF16)
        earlier = sb("earlier", [P, E], BF16)
        newer = sb("newer", [P, E])
        prod = sb("prod", [P, NT, K, E])
        rank = sb("rank", [P, NT, K])
        at_slot = sb("at_slot", [P, NT, K, CAP], BF16)
        who = sb("who", [P, NT, K, 2, E], BF16)
        slot_no = sb("slot_no", [P, CAP], BF16)
        tile_no = sb("tile_no", [P, NT])
        silu = [sb(f"silu{n}", [P, T]) for n in range(RING)]
        hidden = [sb(f"hidden{j}", [P, T]) for j in range(3)]
        table = sb("table", [P, 2, E])
        empty = sb("empty", [P, E])
        zero = sb("zero", [P, P], BF16)

        p_turn = ps("p_turn", [P, T])
        p_gate = ps("p_gate", [P, 2, NT, E])
        p_table = ps("p_table", [P, T])
        p_up = [[ps(f"p_up{n}{g}", [P, T]) for g in range(2)] for n in range(RING)]
        p_z = ps("p_z", [P, 2, D])

        x_loaded = [sem(f"x_loaded{u}") for u in range(2)]
        acc_stored = [sem(f"acc_stored{u}") for u in range(2)]
        rows_stored = [sem(f"rows_stored{u}") for u in range(2)]
        shared_loaded = sem("shared_loaded")
        stats_ready = sem("stats_ready")
        scales_ready = sem("scales_ready")
        xn_ready = sem("xn_ready")
        turned = sem("turned")
        xnT_ready = sem("xnT_ready")
        logits_ready = sem("logits_ready")
        shifted_ready = sem("shifted_ready")
        exp_ready = sem("exp_ready")
        probs_ready = sem("probs_ready")
        picked_ready = sem("picked_ready")
        ranks_ready = sem("ranks_ready")
        slots_ready = sem("slots_ready")
        who_ready = sem("who_ready")
        table_added = sem("table_added")
        up_ready = sem("up_ready")
        silu_ready = sem("silu_ready")
        hidden_ready = sem("hidden_ready")
        z_ready = sem("z_ready")
        acc_ready = sem("acc_ready")
        setup_done = sem("setup_done")

        def loop(eng, chunk):
            for u in range(2):
                chunk(u, 0, u, False)
            with eng.Fori(1, N // 2 - 1) as i:
                for u in range(2):
                    chunk(2 * i + u, i, u, False)
            chunk(N - 2, N // 2 - 1, 0, False)
            chunk(N - 1, N // 2 - 1, 1, True)

        with nc.Block() as block:
            @block.sync
            def _(sp):
                sp.dma_start(x[0][:], src[0]).then_inc(x_loaded[0], 16)
                sp.dma_start(ws1T[:], dram.ws1T).then_inc(shared_loaded, 16)
                sp.dma_start(ws3T[:], dram.ws3T).then_inc(shared_loaded, 16)
                for j in range(3):
                    sp.dma_start(ws2T[0:SJ[j], j, :], dram.ws2T[j * P:j * P + SJ[j], :]).then_inc(shared_loaded, 16)

                def chunk(c, i, u, last):
                    if not last:
                        if u == 0:
                            wait_count(sp, acc_stored[1], 16 * i)
                            sp.dma_start(x[1][:], src[c + 1]).then_inc(x_loaded[1], 16)
                        else:
                            sp.wait_ge(acc_stored[0], 16 * i + 16)
                            sp.dma_start(x[0][:], src[c + 1]).then_inc(x_loaded[0], 16)
                    sp.wait_ge(xn_ready, c + 1)
                    sp.wait_ge(probs_ready, c + 1)
                    sp.dma_start(dram.rows_chunks[c], row[u][:]).then_inc(rows_stored[u], 16)
                    sp.wait_ge(acc_ready, 2 * c + 2)
                    sp.dma_start(acc[c], x[u][:]).then_inc(acc_stored[u], 16)

                loop(sp, chunk)
                for u in range(2):
                    sp.wait_ge(acc_stored[u], 8 * N)
                    sp.wait_ge(rows_stored[u], 8 * N)

            @block.gpsimd
            def _(pool):
                def scales(c):
                    wait_count(pool, xn_ready, c)
                    pool.wait_ge(stats_ready, c + 1)
                    token_scales(nc, pool, mv, rstd, shift, w).then_inc(scales_ready, 1)

                scales(0)
                with pool.Fori(1, N) as c:
                    scales(c)

            @block.scalar
            def _(act):
                def evacuate(c):
                    for h in range(DC):
                        act.wait_ge(turned, DC * c + h + 1)
                        nc.scalar.copy(xnT[:, h, :], p_turn[:]).then_inc(xnT_ready, 1)

                def normalise(c, i, u):
                    wait_count(act, rows_stored[u], 16 * i)
                    act.wait_ge(scales_ready, c + 1)
                    token_normalise(nc, x[u], rstd, shift, row[u]).then_inc(xn_ready, 1)

                normalise(0, 0, 0)
                evacuate(0)

                def write_down(c):
                    act.wait_ge(picked_ready, c + 1)
                    wait_count(act, table_added, c)
                    nc.scalar.activation(who[:, :, :, 0, :].rearrange("p t k e -> p (t k) e"),
                                         pick[:].rearrange("p t k e -> p (t k) e"), ACT.Copy, scale=w.lane[:, 0:1])
                    for t in range(NT):
                        ins = nc.scalar.activation(who[:, t, :, 1, :], pick[:, t, :, :], ACT.Copy,
                                                   scale=tile_no[:, t:t + 1])
                    ins.then_inc(who_ready, 1)

                def chunk(c, i, u, last):
                    act.wait_ge(shifted_ready, c + 1)
                    nc.scalar.activation(expd[:], shifted[:], ACT.Exp).then_inc(exp_ready, 1)
                    for j in range(3):
                        n = (u + j) % RING
                        m = SJ[j]
                        act.wait_ge(hidden_ready, 3 * c + j + 1)
                        act.wait_ge(up_ready, 3 * c + j + 1)
                        nc.scalar.activation(silu[n][0:m, :], p_up[n][0][0:m, :], ACT.Silu).then_inc(silu_ready, 1)
                        if j == 0 and not last:
                            normalise(c + 1, i + u, 1 - u)
                    write_down(c)
                    if not last:
                        evacuate(c + 1)

                loop(act, chunk)

            @block.vector
            def _(dve):
                nc.vector.memset(earlier[:], 0.0)
                nc.vector.memset(zero[:], 0.0)
                nc.vector.tensor_copy(tile_no[:], w.first_tiles[:])
                nc.vector.tensor_copy(slot_no[:], w.iota_slot[:])
                dve.drain()
                dve.sem_inc(hidden_ready, RING)
                dve.sem_inc(setup_done, 1)

                def statistics(c, i, u):
                    dve.wait_ge(x_loaded[u], 16 * i + 16)
                    wait_count(dve, scales_ready, c)
                    token_stats(nc, dve, x[u], stats, mv).then_inc(stats_ready, 1)

                def multiply(c, u, j):
                    n = (u + j) % RING
                    m = SJ[j]
                    dve.wait_ge(silu_ready, 3 * c + j + 1)
                    nc.vector.tensor_tensor(hidden[j][0:m, :], silu[n][0:m, :], p_up[n][1][0:m, :],
                                            ALU.mult).then_inc(hidden_ready, 1)

                def slots(c):
                    wait_count(dve, table_added, c)
                    for t in range(NT):
                        for k in range(K):
                            ins = nc.vector.tensor_scalar(at_slot[:, t, k, :], slot_no[:], rank[:, t, k:k + 1],
                                                          None, ALU.is_equal)
                    ins.then_inc(slots_ready, 1)

                statistics(0, 0, 0)

                def chunk(c, i, u, last):
                    dve.wait_ge(logits_ready, c + 1)
                    nc.vector.tensor_reduce(gmax[:], p_gate[:, 0, :, :], AX.X, ALU.max)
                    dve.drain()
                    nc.vector.tensor_tensor(shifted[:], p_gate[:, 0, :, :],
                                            gmax[:].unsqueeze(2).to_broadcast([P, NT, E]),
                                            ALU.subtract).then_inc(shifted_ready, 1)
                    if not last:
                        statistics(c + 1, i + u, 1 - u)
                    multiply(c, u, 0)
                    dve.wait_ge(exp_ready, c + 1)
                    nc.vector.tensor_reduce(gsum[:], expd[:], AX.X, ALU.add)
                    dve.drain()
                    nc.vector.reciprocal(grec[:], gsum[:])
                    dve.drain()
                    nc.vector.tensor_tensor(row[u][:, :, D:ROW], expd[:],
                                            grec[:].unsqueeze(2).to_broadcast([P, NT, E]),
                                            ALU.mult).then_inc(probs_ready, 1)
                    dve.drain()
                    nc.vector.tensor_tensor(biased[:], row[u][:, :, D:ROW],
                                            w.gate_b[:].unsqueeze(1).to_broadcast([P, NT, E]), ALU.add)
                    dve.drain()
                    for t in range(NT):
                        nc.vector.max(top[:, t, :], biased[:, t, :])
                    dve.drain()
                    for t in range(NT):
                        nc.vector.max_index(topi[:, t, :], top[:, t, :], biased[:, t, :])
                    dve.drain()
                    nc.vector.tensor_copy(topf[:], topi[:, :, 0:K])
                    wait_count(dve, who_ready, c)
                    nc.vector.tensor_tensor(tile_no[:], tile_no[:], w.tiles_per_chunk[:], ALU.add)
                    dve.drain()
                    nc.vector.tensor_tensor(pick[:].rearrange("p t k e -> p (t k) e"),
                                            w.iota_expert[:].unsqueeze(1).to_broadcast([P, NT * K, E]),
                                            topf[:].rearrange("p t k -> p (t k)").unsqueeze(2).to_broadcast([P, NT * K, E]),
                                            ALU.is_equal)
                    dve.drain()
                    with nc.allow_low_precision("a sum of at most one 1"):
                        nc.vector.tensor_reduce(picked[:], pick[:].rearrange("p t k e -> p t e k"), AX.X,
                                                ALU.add).then_inc(picked_ready, 1)
                    multiply(c, u, 1)
                    multiply(c, u, 2)
                    dve.wait_ge(ranks_ready, c + 1)
                    nc.vector.tensor_tensor(prod[:], pick[:],
                                            p_gate[:, 1, :, :].unsqueeze(2).to_broadcast([P, NT, K, E]), ALU.mult)
                    nc.vector.tensor_reduce(newer[:], picked[:].rearrange("p t e -> p e t"), AX.X, ALU.add)
                    dve.drain()
                    nc.vector.tensor_reduce(rank[:], prod[:], AX.X, ALU.add)
                    nc.vector.tensor_tensor(earlier[:], earlier[:], newer[:], ALU.add)
                    for r in range(2):
                        dve.wait_ge(z_ready, 2 * c + r + 1)
                        nc.vector.scalar_tensor_tensor(x[u][:, 2 * r:2 * r + 2, :], p_z[:], 0.5,
                                                       x[u][:, 2 * r:2 * r + 2, :], ALU.mult,
                                                       ALU.add).then_inc(acc_ready, 1)
                    slots(c)

                loop(dve, chunk)
                dve.wait_ge(table_added, N)
                nc.vector.tensor_copy(table[:].rearrange("p a e -> p (a e)"), p_table[:, 0:2 * E])
                dve.drain()
                nc.vector.tensor_scalar(empty[:], table[:, 1, :], 0.0, w.dummy_row[:, 0:1], ALU.is_equal, ALU.mult)
                nc.vector.scalar_tensor_tensor(table[:, 0, :], table[:, 1, :], float(P), table[:, 0, :],
                                               ALU.mult, ALU.add)
                dve.drain()
                nc.vector.scalar_tensor_tensor(w.slot_token[:], table[:, 0, :], float(-P), empty[:],
                                               ALU.add, ALU.add)

            @block.tensor
            def _(pe):
                def turn(c, u, h):
                    pe.wait_ge(xn_ready, c + 1)
                    wait_count(pe, xnT_ready, DC * c + h)
                    for t in range(NT):
                        last = nc.tensor.transpose(p_turn[:, t * P:(t + 1) * P], row[u][:, t, h * P:(h + 1) * P],
                                                   w.ident[:])
                    last.then_inc(turned, 1)

                pe.wait_ge(setup_done, 1)
                pe.wait_ge(shared_loaded, 16 * 5)
                nc.tensor.matmul(p_table[:], zero[:], w.ones_row[:], start=True, stop=True)
                for h in range(DC):
                    turn(0, 0, h)

                def add_to_table(c):
                    pe.wait_ge(slots_ready, c + 1)
                    pe.wait_ge(who_ready, c + 1)
                    for t in range(NT):
                        for k in range(K):
                            ins = nc.tensor.matmul(p_table[:, 0:2 * E], at_slot[:, t, k, :],
                                                   who[:, t, k, :, :].rearrange("p a e -> p (a e)"),
                                                   start=False, stop=True, skip_group_check=True)
                    ins.then_inc(table_added, 1)

                def chunk(c, i, u, last):
                    pe.wait_ge(xnT_ready, DC * c + DC)
                    wait_count(pe, shifted_ready, c)
                    for t in range(NT):
                        for h in range(DC):
                            ins = nc.tensor.matmul(p_gate[:, 0, t, :], xnT[:, h, t * P:(t + 1) * P], w.gateT[:, h, :],
                                                   start=(h == 0), stop=(h == DC - 1))
                    ins.then_inc(logits_ready, 1)
                    for j in range(3):
                        n = (u + j) % RING
                        m = SJ[j]
                        pe.wait_ge(hidden_ready, 3 * c + j + 1)
                        for g, ws in enumerate((ws1T, ws3T)):
                            for h in range(DC):
                                ins = nc.tensor.matmul(p_up[n][g][0:m, :], ws[:, h, j * P:j * P + m], xnT[:, h, :],
                                                       start=(h == 0), stop=(h == DC - 1))
                        ins.then_inc(up_ready, 1)
                        if j == 1 and not (isinstance(c, int) and c == 0):
                            add_to_table(c - 1)
                    if not last:
                        turn(c + 1, 1 - u, 0)
                    pe.wait_ge(picked_ready, c + 1)
                    for t in range(NT):
                        nc.tensor.matmul(p_gate[:, 1, t, :], w.before[:], picked[:, t, :], start=True, stop=False)
                        for s in range(t):
                            nc.tensor.matmul(p_gate[:, 1, t, :], w.ones[:], picked[:, s, :], start=False, stop=False)
                        ins = nc.tensor.matmul(p_gate[:, 1, t, :], w.ones[:], earlier[:], start=False, stop=True)
                    ins.then_inc(ranks_ready, 1)
                    for r in range(2):
                        pe.wait_ge(hidden_ready, 3 * c + 3 + RING)
                        wait_count(pe, acc_ready, 2 * c + r)
                        for s in range(2):
                            t = 2 * r + s
                            for j in range(3):
                                m = SJ[j]
                                ins = nc.tensor.matmul(p_z[:, s, :], hidden[j][0:m, t * P:(t + 1) * P],
                                                       ws2T[0:m, j, :], start=(j == 0), stop=(j == 2))
                        ins.then_inc(z_ready, 1)
                        if r == 0 and not last:
                            turn(c + 1, 1 - u, 1)

                loop(pe, chunk)
                add_to_table(N - 1)

def experts(nc, w, dram, acc, tag):
    WR = 4
    with ExitStack() as ctx:
        def sb(name, shape, dt=F32):
            return ctx.enter_context(nc.sbuf_tensor(f"{tag}_{name}", shape, dt))

        def ps(name, shape, dt=F32):
            return ctx.enter_context(nc.psum_tensor(f"{tag}_{name}", shape, dt))

        def sem(name):
            return ctx.enter_context(nc.semaphore(f"{tag}_{name}"))

        w13 = [sb(f"w13_{s}", [P, DC, SI]) for s in range(WR)]
        w2 = [sb(f"w2_{s}", [IH, 2, D]) for s in range(WR)]
        got = [sb(f"got{s}", [P, ROW]) for s in range(WR)]
        y = [sb(f"y{s}", [P, D]) for s in range(WR)]
        xT = [sb(f"xT{s}", [P, DC, CAP]) for s in range(2)]
        silu = [sb(f"silu{s}", [IH, 2, CAP]) for s in range(2)]
        hidden = [sb(f"hidden{s}", [IH, 2, CAP]) for s in range(2)]
        weight = sb("weight", [P, WR])

        p_turn = [ps(f"p_turn{s}", [P, DC, CAP]) for s in range(2)]
        p_up = [ps(f"p_up{s}", [P, 4, CAP]) for s in range(2)]
        p_y = [ps(f"p_y{s}", [P, D]) for s in range(2)]

        weights_loaded = [sem(f"weights_loaded{s}") for s in range(WR)]
        gathered = [sem(f"gathered{s}") for s in range(WR)]
        added = sem("added")
        y_free = sem("y_free")
        turned = sem("turned")
        xT_ready = sem("xT_ready")
        up_ready = sem("up_ready")
        silu_ready = sem("silu_ready")
        hidden_ready = sem("hidden_ready")
        y_ready = sem("y_ready")
        y_scaled = sem("y_scaled")

        with nc.Block() as block:
            @block.sync
            def _(sp):
                def load(e, q, s):
                    sp.dma_start(w13[s][:], dram.w13[e]).then_inc(weights_loaded[s], 16)
                    sp.dma_start(w2[s][:], dram.w2[e]).then_inc(weights_loaded[s], 16)

                for s in range(WR):
                    load(s, 0, s)
                with sp.Fori(1, E // WR) as q:
                    for s in range(WR):
                        sp.wait_ge(y_ready, WR * q + s - WR + 1)
                        load(WR * q + s, q, s)

            @block.gpsimd
            def _(pool):
                def gather(e, s):
                    nc.gpsimd.indirect_dma_start(
                        out=got[s][:], out_offset=None, in_=dram.rows,
                        in_offset=bass.IndirectOffsetOnAxis(ap=w.slot_token[:, e:e + 1].bitcast(U32), axis=0),
                    ).then_inc(gathered[s], 16)

                def add(e, s):
                    nc.gpsimd.indirect_dma_start(
                        out=acc, out_offset=bass.IndirectOffsetOnAxis(
                            ap=w.slot_token[:, e:e + 1].bitcast(U32), axis=0),
                        in_=y[s][:], in_offset=None, compute_op=ALU.add).then_inc(added, 16)

                pool.sem_inc(y_free, WR)
                for e in range(WR):
                    gather(e, e)
                for e in range(E):
                    pool.wait_ge(y_scaled, e + 1)
                    if e > 0:
                        pool.wait_ge(added, 16 * e)
                        pool.sem_inc(y_free, 1)
                    add(e, e % WR)
                    if e + WR < E:
                        gather(e + WR, e % WR)
                pool.wait_ge(added, 16 * E)

            @block.scalar
            def _(act):
                def silus(i):
                    for s in range(2):
                        wait_count(act, hidden_ready, 2 * i)
                        act.wait_ge(up_ready, 2 * i + s + 1)
                        nc.scalar.activation(silu[s][:], p_up[s][0:IH, 0:2, :], ACT.Silu).then_inc(silu_ready, 1)

                silus(0)
                with act.Fori(1, E // 2) as i:
                    silus(i)

            @block.vector
            def _(dve):
                def bring(e, q, s):
                    dve.wait_ge(turned, e + 1)
                    nc.vector.tensor_copy(xT[s % 2][:], p_turn[s % 2][:]).then_inc(xT_ready, 1)

                def multiply(e, q, s):
                    dve.wait_ge(silu_ready, e + 1)
                    nc.vector.tensor_tensor(hidden[s % 2][:], silu[s % 2][:], p_up[s % 2][0:IH, 2:4, :],
                                            ALU.mult).then_inc(hidden_ready, 1)

                def scale(e, q, s):
                    dve.wait_ge(y_ready, e + 1)
                    dve.wait_ge(y_free, e + 1)
                    nc.vector.tensor_scalar(y[s][:], p_y[s % 2][:], got[s][:, bass.ds(e + D, 1)], 0.5,
                                            ALU.mult, ALU.mult).then_inc(y_scaled, 1)

                pipeline(dve, bring, multiply, scale)

            @block.tensor
            def _(pe):
                def turn(e, q, s):
                    pe.wait_ge(gathered[s], 16 * q + 16)
                    for h in range(DC):
                        ins = nc.tensor.transpose(p_turn[s % 2][:, h, :], got[s][:, h * P:(h + 1) * P], w.ident[:])
                    ins.then_inc(turned, 1)

                def up(e, q, s):
                    pe.wait_ge(weights_loaded[s], 32 * q + 32)
                    pe.wait_ge(xT_ready, e + 1)
                    for g in range(4):
                        for h in range(DC):
                            ins = nc.tensor.matmul(p_up[s % 2][0:IH, g, :], w13[s][:, h, g * IH:(g + 1) * IH],
                                                   xT[s % 2][:, h, :], start=(h == 0), stop=(h == DC - 1))
                    ins.then_inc(up_ready, 1)

                def down(e, q, s):
                    pe.wait_ge(hidden_ready, e + 1)
                    for g in range(2):
                        ins = nc.tensor.matmul(p_y[s % 2][:], hidden[s % 2][:, g, :], w2[s][:, g, :],
                                               start=(g == 0), stop=(g == 1))
                    ins.then_inc(y_ready, 1)

                pipeline(pe, turn, up, down)



def pipeline(eng, first, second, third):
    first(0, 0, 0)
    first(1, 0, 1)
    second(0, 0, 0)
    with eng.Fori(0, E // 4 - 1) as q:
        for s in range(4):
            first(4 * q + s + 2, q + (s + 2) // 4, (s + 2) % 4)
            second(4 * q + s + 1, q + (s + 1) // 4, (s + 1) % 4)
            third(4 * q + s, q, s)
    last = E // 4 - 1
    for s in range(3):
        if s < 2:
            first(E - 2 + s, last, s + 2)
        second(E - 3 + s, last, s + 1)
        third(E - 4 + s, last, s)
    third(E - 1, last, 3)

HIGH, MIDDLE, LOW = range(3)
Q_SLOTS = [HIGH, HIGH, MIDDLE, HIGH, LOW, MIDDLE]
K_SLOTS = [HIGH, MIDDLE, HIGH, LOW, HIGH, MIDDLE]
SR = HD * len(Q_SLOTS)
MASK = 4
TOP = 3
QUADS = H // 4
HP = 32
PAGE = 64
SCALE = HD ** -0.5
SCORE_BANKS, MISC_BANKS, OUT_BANKS = 4, 2, 2

GROUPS = "ABC"
GROUP_BANKS = {"A": 4, "B": 4, "C": 2}


def score_pieces(group, n):
    if group == "A":
        return [(n, 3, 0, 512)]
    if group == "B":
        return [(n, 2, 0, 384), (n, 0, 384, 128)]
    return [(2 * n, 1, 0, 256), (2 * n + 1, 1, 256, 256)]


def banks_of(kind, quad, group):
    return [(kind, quad, group, k) for k in range(GROUP_BANKS[group])]


def quads_maxima(quads):
    return [s for g in quads for x in GROUPS for s in banks_of("S1", g, x)]


PROJECT = [("XT", 0), ("XT", 1), ("LAT", 0), ("Q", 0), ("Q", 1), ("HIGH", 0), ("K", 0), ("HIGH", 1), ("SPLIT", 0),
           ("K", 1), ("SPLIT", 1), ("HIGH", 2), ("STATS",), ("HIGH", 3), ("SPLIT", 2), ("SPLIT", 3), ("NORM",)]
MAXIMA = quads_maxima([0, 1]) + [("MAX", 0)] + quads_maxima([2, 3]) + [("MAX", 1)]


def quads_probs(first, last):
    steps = []
    for g in range(first, last):
        steps += banks_of("S2", g, "A")
        if g > first:
            steps += [("PV", g - 1, "C")]
        steps += banks_of("S2", g, "B") + [("PV", g, "A")]
        if g > first:
            steps += [("OUT", g - 1)]
        steps += banks_of("S2", g, "C") + [("PV", g, "B")]
    return steps + [("PV", last - 1, "C")]


OUTPUTS = (quads_probs(0, QUADS) + [("STACK", 0), ("STACK", 1), ("OUT", QUADS - 1), ("V", 0), ("V", 1),
                                    ("AT", 0), ("AT", 1), ("WO", 0), ("WO", 1)])
PE_TIME = {"S1": 2, "S2": 2, "PV": 9, "OUT": 9, "AT": 9, "WO": 17, "XT": 9, "LAT": 17, "Q": 17, "K": 9, "V": 9}


def spread(main, side, first, last):
    out, side, done = [], list(side), 0
    total, count, given = sum(PE_TIME.get(s[0], 0) for s in main), len(side), 0
    for step in main:
        out.append(step)
        done += PE_TIME.get(step[0], 0)
        while side and given < count * (done / total - first) / (last - first):
            out.append(side.pop(0))
            given += 1
    return out + side


def without(steps, *kinds):
    return [s for s in steps if s[0] not in kinds]


AHEAD = [("STACK", 0), ("STACK", 1), ("V", 0), ("V", 1)]
FIRST_TURN = PROJECT + AHEAD
SECOND_TURN = spread(MAXIMA, PROJECT, 0.0, 0.6) + AHEAD
TURN = spread(spread(OUTPUTS, PROJECT, 0.0, 0.7), MAXIMA, 0.03, 0.97)
TURN_WITHOUT_NORM = without(TURN, "STATS", "NORM")
NEXT_TO_LAST_TURN = spread(without(OUTPUTS, "STACK", "NORM", "V"), MAXIMA, 0.03, 0.97)
LAST_TURN = without(OUTPUTS, "STACK", "NORM", "V")

MISC_STEPS = {"XT", "Q", "LAT", "K", "V", "OUT", "AT", "WO", "MAX"}


def count_misc(steps):
    return sum(s[0] in MISC_STEPS for s in steps)


def count_scores(steps):
    return sum(s[0] in ("S1", "S2") for s in steps)


class Places:

    def __init__(self, banks, earlier):
        self.before = [sum(number * len(range(n, uses, banks)) for uses, number in earlier) for n in range(banks)]
        self.banks, self.n = banks, 0

    def next(self):
        bank, used = self.n % self.banks, self.before[self.n % self.banks] + self.n // self.banks
        self.n += 1
        return bank, used


def attention(nc, w, dram, src, dst, tag):
    with ExitStack() as ctx:
        def sb(name, shape, dt=F32):
            return ctx.enter_context(nc.sbuf_tensor(f"{tag}_{name}", shape, dt))

        def ps(name, shape, dt=F32):
            return ctx.enter_context(nc.psum_tensor(f"{tag}_{name}", shape, dt))

        def sem(name):
            return ctx.enter_context(nc.semaphore(f"{tag}_{name}"))

        wq = sb("wq", [P, DC, D])
        w_down = sb("w_down", [P, DC, P])
        wk, wv = sb("wk", [P, D]), sb("wv", [P, D])
        wo = sb("wo", [P, DC, D])
        cos, sin = sb("cos", [P, T]), sb("sin", [P, T])
        ident16 = sb("ident16", [P, P], BF16)

        x = sb("x", [P, NT, D])
        residual = sb("residual", [P, NT, D])
        stats, mv = sb("stats", [P, NT, 6]), sb("mv", [P, NT, 2])
        rstd, shift = sb("rstd", [P, NT]), sb("shift", [P, NT])
        xnT = sb("xnT", [P, DC, T])
        latT = sb("latT", [P, T])
        swapped = [sb(f"swapped{n}", [P, T]) for n in range(2)]
        qk = [sb(f"qk{r}", [P, T]) for r in range(4)]
        parts = [sb(f"parts{r}", [P, 3, T], BF16) for r in range(4)]
        qs = [sb(f"qs{u}", [P, H, T], BF16) for u in range(2)]
        ks = [sb(f"ks{u}", [P, H, T], BF16) for u in range(2)]
        v = [sb(f"v{u}", [P, NT, H, HP]) for u in range(2)]
        probs = [sb(f"probs{n}", [P, T]) for n in range(10)]
        outT = [sb(f"outT{n}", [P, T]) for n in range(OUT_BANKS)]
        rsum = sb("rsum", [P, NT, 4])
        attn = sb("attn", [P, NT, D])
        attnT = xnT
        smax = sb("smax", [P, NT, H])
        smax_rest = sb("smax_rest", [P, NT, H])
        smax_parts = [sb(f"smax_parts{n}", [P, NT, P], BF16) for n in range(2)]
        smaxT = [sb(f"smaxT{n}", [TOP * H // 2, T], BF16) for n in range(2)]

        p_score = [ps(f"p_score{n}", [P, T]) for n in range(SCORE_BANKS)]
        p_out = [ps(f"p_out{n}", [P, T]) for n in range(OUT_BANKS)]
        p_misc = [ps(f"p_misc{n}", [P, T]) for n in range(MISC_BANKS)]

        pairs_ready = sem("pairs_ready")
        setup_loaded, setup_done = sem("setup_loaded"), sem("setup_done")
        x_loaded = sem("x_loaded")
        residual_loaded = sem("residual_loaded")
        stats_ready, scales_ready, xn_ready = sem("stats_ready"), sem("scales_ready"), sem("xn_ready")
        rope_ready, high_ready, rest_ready = sem("rope_ready"), sem("high_ready"), sem("rest_ready")
        middle_ready, low_ready = sem("middle_ready"), sem("low_ready")
        parts_stored = [sem(f"{name}_parts_stored") for name in "qk"]
        stack_loaded = sem("stack_loaded")
        misc_ready = [sem(f"misc_ready{n}") for n in range(MISC_BANKS)]
        misc_free = [sem(f"misc_free{n}") for n in range(MISC_BANKS)]
        score_ready = [sem(f"score_ready{n}") for n in range(SCORE_BANKS)]
        score_free = [sem(f"score_free{n}") for n in range(SCORE_BANKS)]
        smax_parts_ready = sem("smax_parts_ready")
        smax_stored = [sem(f"smax_stored{e}") for e in range(2)]
        smax_loaded = [sem(f"smax_loaded{e}") for e in range(2)]
        quad_done, outT_ready = sem("quad_done"), sem("outT_ready")
        result_stored = sem("result_stored")

        def places(b):
            if isinstance(b, int) and b < 0:
                earlier = [(FIRST_TURN, b + 2)]
            elif isinstance(b, int) and b == B - 1:
                earlier = [(FIRST_TURN, 1), (SECOND_TURN, 1), (TURN, B - 2), (NEXT_TO_LAST_TURN, 1)]
            else:
                earlier = [(FIRST_TURN, 1), (SECOND_TURN, 1), (TURN, b)]
            return (Places(MISC_BANKS, [(count_misc(steps), number) for steps, number in earlier]),
                    Places(SCORE_BANKS, [(count_scores(steps), number) for steps, number in earlier]))

        def turns(eng, turn):
            turn(-2, 0, FIRST_TURN, *places(-2))
            turn(-1, 1, SECOND_TURN, *places(-1))
            with eng.Fori(0, B // 2 - 2) as i:
                for u in range(2):
                    turn(2 * i + u, u, TURN, *places(2 * i + u))
            turn(B - 4, 0, TURN, *places(B - 4))
            turn(B - 3, 1, TURN_WITHOUT_NORM, *places(B - 3))
            turn(B - 2, 0, NEXT_TO_LAST_TURN, *places(B - 2))
            turn(B - 1, 1, LAST_TURN, *places(B - 1))

        with nc.Block() as block:
            @block.sync
            def _(sp):
                for to, fro in ((wq[:], dram.wq), (w_down[:], dram.w_down), (wk[:], dram.wk), (wv[:], dram.wv),
                                (wo[:], dram.wo), (cos[:], dram.cos), (sin[:], dram.sin),
                                (residual[SR:SR + MASK, :, :].rearrange("p t d -> p (t d)"), dram.mask)):
                    sp.dma_start(to, fro).then_inc(setup_loaded, 16)
                sp.dma_start(x[:], src[0]).then_inc(x_loaded, 16)
                sp.wait_ge(setup_done, 1)
                sp.dma_start(residual[:], src[0]).then_inc(residual_loaded, 16)

                def store_parts(r, j, u):
                    if r == 0:
                        wait_count(sp, stack_loaded, 192 * (j - 1))
                    sp.wait_ge(low_ready, 4 * j + r + 1)
                    sp.dma_start(dram.parts[u, r // 2, :, (r % 2) * P:(r % 2 + 1) * P, :].rearrange("s p t -> p s t"),
                                 parts[r][:]).then_inc(parts_stored[r // 2], 16)

                def stack(kind, j, u):
                    sp.wait_ge(parts_stored[kind], 32 * j + 32)
                    to, slots = ((qs, Q_SLOTS), (ks, K_SLOTS))[kind]
                    for s, part in enumerate(slots):
                        sp.dma_start(to[u][s * HD:(s + 1) * HD, :, :],
                                     dram.parts[u, kind, part, :, :].rearrange("(h d) t -> d h t", d=HD)
                                     ).then_inc(stack_loaded, 16)

                def turn(b, u, steps, misc, scores):
                    n, j = b + 1, b + 2
                    last_scores = None
                    for step in steps:
                        if step[0] in MISC_STEPS:
                            m, used = misc.next()
                        if step[0] in ("S1", "S2"):
                            place = scores.next()
                            if step[0] == "S2":
                                last_scores = place
                        if step == ("XT", 1) and ("STATS",) in steps:
                            sp.wait_ge(misc_free[m], used + 1)
                            sp.dma_start(x[:], src[j + 1]).then_inc(x_loaded, 16)
                        if step[0] == "SPLIT":
                            store_parts(step[1], j, u)
                        elif step[0] == "STACK":
                            if last_scores is not None and step[1] == 0:
                                sp.wait_ge(score_ready[last_scores[0]], last_scores[1] + 1)
                            stack(step[1], j, u)
                        elif step[0] == "MAX":
                            e = step[1]
                            sp.wait_ge(misc_free[m], used + 1)
                            sp.dma_start(dram.smax[1 - u, e], smaxT[e][:]).then_inc(smax_stored[e], 16)
                            sp.wait_ge(smax_stored[e], 16 * n + 16)
                            sp.dma_start(qs[1 - u][SR + MASK:SR + MASK + TOP, e * H // 2:(e + 1) * H // 2, :],
                                         dram.smax[1 - u, e].rearrange("(s h) t -> s h t", s=TOP)
                                         ).then_inc(smax_loaded[e], 16)
                        elif step == ("WO", 1):
                            sp.wait_ge(misc_free[m], used + 1)
                            sp.dma_start(dst[b], residual[:]).then_inc(result_stored, 16)
                            if steps is not LAST_TURN:
                                sp.wait_ge(result_stored, 16 * b + 16)
                                sp.dma_start(residual[:], src[b + 1]).then_inc(residual_loaded, 16)

                turns(sp, turn)
                sp.wait_ge(result_stored, 16 * B)

            @block.gpsimd
            def _(pool):
                def scales(n):
                    wait_count(pool, xn_ready, n)
                    pool.wait_ge(stats_ready, n + 1)
                    token_scales(nc, pool, mv, rstd, shift, w).then_inc(scales_ready, 1)

                def turn(b, u, steps, misc, scores):
                    n, j = b + 1, b + 2
                    for step in steps:
                        if step[0] in ("Q", "K"):
                            r = step[1] + (2 if step[0] == "K" else 0)
                            pool.wait_ge(pairs_ready, 4 * j + r + 1)
                            nc.gpsimd.tensor_tensor(swapped[r % 2][:], swapped[r % 2][:], sin[:], ALU.mult)
                            pool.drain()
                            nc.gpsimd.tensor_tensor(qk[r][:], qk[r][:], swapped[r % 2][:], ALU.add
                                                    ).then_inc(rope_ready, 1)
                        elif step[0] == "SPLIT":
                            r = step[1]
                            pool.wait_ge(middle_ready, 4 * j + r + 1)
                            nc.gpsimd.tensor_tensor(parts[r][:, LOW, :], qk[r][:], parts[r][:, MIDDLE, :],
                                                    ALU.subtract).then_inc(low_ready, 1)
                        elif step[0] == "STATS":
                            scales(j + 1)

                scales(0)
                turns(pool, turn)

            @block.scalar
            def _(act):
                def normalise(n):
                    act.wait_ge(scales_ready, n + 1)
                    token_normalise(nc, x, rstd, shift, x).then_inc(xn_ready, 1)

                def turn(b, u, steps, misc, scores):
                    n, j = b + 1, b + 2
                    def bank():
                        m, used = misc.next()
                        return m, used + 1

                    for step in steps:
                        kind = step[0]
                        if kind == "S1":
                            scores.next()
                        elif kind == "S2":
                            s, used = scores.next()
                            act.wait_ge(score_ready[s], used + 1)
                            to = probs[{"A": 0, "B": 4, "C": 8}[step[2]] + step[3]]
                            nc.scalar.activation(to[:], p_score[s][:], ACT.Exp, scale=SCALE
                                                 ).then_inc(score_free[s], 1)
                        elif kind == "PV" and step[2] == "C":
                            act.wait_ge(quad_done, QUADS * b + step[1] + 1)
                            nc.scalar.copy(outT[step[1] % OUT_BANKS][:], p_out[step[1] % OUT_BANKS][:]
                                           ).then_inc(outT_ready, 1)
                        elif kind == "XT":
                            m, use = bank()
                            act.wait_ge(misc_ready[m], use)
                            nc.scalar.copy(xnT[:, step[1], :], p_misc[m][:]).then_inc(misc_free[m], 1)
                        elif kind == "LAT":
                            m, use = bank()
                            act.wait_ge(misc_ready[m], use)
                            nc.scalar.copy(latT[:], p_misc[m][:]).then_inc(misc_free[m], 1)
                        elif kind == "V":
                            m, use = bank()
                            act.wait_ge(misc_ready[m], use)
                            for s in range(2):
                                ins = nc.scalar.copy(v[u][:, 2 * step[1] + s, :, 0:HD],
                                                     p_misc[m][:, s * D:(s + 1) * D].rearrange("p (h d) -> p h d", d=HD))
                            ins.then_inc(misc_free[m], 1)
                        elif kind == "AT":
                            m, use = bank()
                            act.wait_ge(misc_ready[m], use)
                            nc.scalar.copy(attnT[:, step[1], :], p_misc[m][:]).then_inc(misc_free[m], 1)
                        elif kind == "MAX":
                            m, use = bank()
                            e = step[1]
                            wait_count(act, smax_stored[e], 16 * n)
                            act.wait_ge(misc_ready[m], use)
                            nc.scalar.copy(smaxT[e][:], p_misc[m][0:TOP * H // 2, 0:T // 2].bitcast(BF16)
                                           ).then_inc(misc_free[m], 1)
                        elif kind in MISC_STEPS:
                            misc.next()
                        if kind == "HIGH":
                            r = step[1]
                            wait_count(act, parts_stored[r // 2], 32 * j)
                            act.wait_ge(rope_ready, 4 * j + r + 1)
                            nc.scalar.copy(parts[r][:, HIGH, :], qk[r][:]).then_inc(high_ready, 1)
                        elif kind == "SPLIT":
                            r = step[1]
                            act.wait_ge(rest_ready, 4 * j + r + 1)
                            nc.scalar.copy(parts[r][:, MIDDLE, :], qk[r][:]).then_inc(middle_ready, 1)
                        elif kind == "NORM":
                            normalise(j + 1)

                normalise(0)
                act.wait_ge(setup_done, 1)
                turns(act, turn)

            @block.vector
            def _(dve):
                dve.wait_ge(setup_loaded, 16 * 8)
                nc.vector.tensor_copy(ident16[:], w.ident[:])
                for e in range(2):
                    nc.vector.memset(smax_parts[e][:], 0.0)
                for u in range(2):
                    nc.vector.memset(v[u][:], 0.0)
                    nc.vector.memset(ks[u][SR:SR + MASK + TOP, :, :], 1.0)
                dve.drain()
                for u in range(2):
                    nc.vector.memset(v[u][:, :, :, HD:HD + 1], 1.0)
                    for to, row in ((qs, 0), (ks, 1)):
                        nc.vector.tensor_copy(
                            to[u][SR:SR + MASK, :, :],
                            residual[SR:SR + MASK, 2 * row:2 * row + 2, :].rearrange("p t d -> p (t d)"
                                                                                    ).unsqueeze(1).to_broadcast([MASK, H, T]))
                dve.drain()
                dve.sem_inc(setup_done, 1)
                swap_pairs = [i ^ 1 for i in range(32)]

                def statistics(n):
                    dve.wait_ge(x_loaded, 16 * n + 16)
                    wait_count(dve, scales_ready, n)
                    token_stats(nc, dve, x, stats, mv).then_inc(stats_ready, 1)

                def turn(b, u, steps, misc, scores):
                    n, j = b + 1, b + 2
                    for step in steps:
                        kind = step[0]
                        m, use = misc.next() if kind in MISC_STEPS else (None, None)
                        if kind == "S2":
                            scores.next()
                        elif kind == "S1":
                            _, g, group, k = step
                            s, used = scores.next()
                            dve.wait_ge(score_ready[s], used + 1)
                            if group == "C":
                                ins = nc.vector.tensor_reduce(
                                    smax[:, 1, 4 * g + 2 * k:4 * g + 2 * k + 2],
                                    p_score[s][:].rearrange("p (h t) -> p h t", h=2), AX.X, ALU.max)
                            else:
                                for h, t, at, length in score_pieces(group, k):
                                    ins = nc.vector.tensor_reduce(smax[:, t, 4 * g + h:4 * g + h + 1],
                                                                  p_score[s][:, at:at + length], AX.X, ALU.max)
                            ins.then_inc(score_free[s], 1)
                        elif kind in ("Q", "K"):
                            r = step[1] + (2 if kind == "K" else 0)
                            wait_count(dve, low_ready, 4 * j)
                            wait_count(dve, rope_ready, 4 * j + max(r - 1, 0))
                            dve.wait_ge(misc_ready[m], use + 1)
                            nc.vector.tensor_tensor(qk[r][:], p_misc[m][:], cos[:], ALU.mult)
                            nc.vector.stream_shuffle(swapped[r % 2][:], p_misc[m][:], swap_pairs)
                            dve.drain()
                            dve.sem_inc(misc_free[m], 1)
                            dve.sem_inc(pairs_ready, 1)
                        elif kind == "SPLIT":
                            r = step[1]
                            dve.wait_ge(high_ready, 4 * j + r + 1)
                            nc.vector.tensor_tensor(qk[r][:], qk[r][:], parts[r][:, HIGH, :],
                                                    ALU.subtract).then_inc(rest_ready, 1)
                        elif kind == "STATS":
                            statistics(j + 1)
                        elif kind == "MAX":
                            e = step[1]
                            low, high = e * H // 2, (e + 1) * H // 2
                            top, rest, part = smax[:, :, low:high], smax_rest[:, :, low:high], smax_parts[e]
                            dve.drain()
                            nc.vector.tensor_scalar(top, top, -1.0, None, ALU.mult)
                            dve.drain()
                            nc.vector.tensor_copy(part[:, :, 0:H // 2], top)
                            dve.drain()
                            nc.vector.tensor_tensor(rest, top, part[:, :, 0:H // 2], ALU.subtract)
                            dve.drain()
                            nc.vector.tensor_copy(part[:, :, H // 2:H], rest)
                            dve.drain()
                            nc.vector.tensor_tensor(part[:, :, H:3 * H // 2], rest, part[:, :, H // 2:H], ALU.subtract
                                                    ).then_inc(smax_parts_ready, 1)
                        elif kind == "OUT":
                            g = step[1]
                            out = p_misc[m][:].rearrange("p (t h c) -> p t h c", t=NT, h=4)
                            dve.wait_ge(misc_ready[m], use + 1)
                            nc.vector.reciprocal(rsum[:], out[:, :, :, HD])
                            dve.drain()
                            nc.vector.tensor_tensor(
                                attn[:, :, g * 4 * HD:(g + 1) * 4 * HD].rearrange("p t (h d) -> p t h d", d=HD),
                                out[:, :, :, 0:HD], rsum[:].unsqueeze(3).to_broadcast([P, NT, 4, HD]),
                                ALU.mult).then_inc(misc_free[m], 1)
                            dve.drain()
                        elif kind == "WO":
                            r = step[1]
                            dve.wait_ge(residual_loaded, 16 * b + 16)
                            dve.wait_ge(misc_ready[m], use + 1)
                            nc.vector.tensor_tensor(residual[:, 2 * r:2 * r + 2, :],
                                                    p_misc[m][:].rearrange("p (t d) -> p t d", t=2),
                                                    residual[:, 2 * r:2 * r + 2, :], ALU.add
                                                    ).then_inc(misc_free[m], 1)

                statistics(0)
                turns(dve, turn)

            @block.tensor
            def _(pe):
                pe.wait_ge(setup_done, 1)

                def turn(b, u, steps, misc, scores):
                    n, j = b + 1, b + 2
                    def take_misc():
                        m, used = misc.next()
                        wait_count(pe, misc_free[m], used)
                        freed[step] = m, used + 1
                        return m

                    def wait_read(of):
                        pe.wait_ge(misc_free[freed[of][0]], freed[of][1])

                    def take_score():
                        s, used = scores.next()
                        wait_count(pe, score_free[s], used)
                        return s

                    freed = {}
                    for step in steps:
                        kind = step[0]
                        if kind == "S1":
                            _, g, group, k = step
                            if (g, group, k) == (0, "A", 0):
                                pe.wait_ge(stack_loaded, 192 * n + 192)
                            s = take_score()
                            for h, t, at, length in score_pieces(group, k):
                                ins = nc.tensor.matmul(p_score[s][:, at:at + length],
                                                       qs[1 - u][0:SR + MASK, 4 * g + h, t * P:(t + 1) * P],
                                                       ks[1 - u][0:SR + MASK, 4 * g + h, 0:length],
                                                       start=True, stop=True)
                            ins.then_inc(score_ready[s], 1)
                        elif kind == "S2":
                            _, g, group, k = step
                            if group == "A" and k == 0 and g % 2 == 0:
                                pe.wait_ge(smax_loaded[g // 2], 16 * b + 16)
                            s = take_score()
                            for h, back, at, length in score_pieces(group, k):
                                t = NT - 1 - back
                                ins = nc.tensor.matmul(p_score[s][:, at:at + length],
                                                       ks[u][0:SR + MASK + TOP, 4 * g + h, t * P:(t + 1) * P],
                                                       qs[u][0:SR + MASK + TOP, 4 * g + h, t * P:T],
                                                       start=True, stop=True)
                            ins.then_inc(score_ready[s], 1)
                            freed[g, group] = s, scores.before[s] + (scores.n - 1) // SCORE_BANKS + 1
                        elif kind == "PV":
                            g, group = step[1:]
                            pe.wait_ge(score_free[freed[step[1:]][0]], freed[step[1:]][1])
                            for piece in range(2 if group == "B" else 1):
                                for h in range(4):
                                    k = {"A": h, "B": 4 + h, "C": 8 + h // 2}[group]
                                    of = score_pieces(group, h // 2 if group == "C" else h)
                                    _, back, at, length = of[h % 2 if group == "C" else piece]
                                    t = NT - 1 - back
                                    ins = nc.tensor.matmul(p_out[g % OUT_BANKS][h * HP:(h + 1) * HP, t * P:T],
                                                           v[u][:, t, 4 * g + h, :], probs[k][:, at:at + length],
                                                           start=(group == "A"), stop=True,
                                                           skip_group_check=True)
                            if group == "C":
                                ins.then_inc(quad_done, 1)
                        elif kind == "OUT":
                            g = step[1]
                            pe.wait_ge(outT_ready, QUADS * b + g + 1)
                            m = take_misc()
                            for t in range(NT):
                                ins = nc.tensor.transpose(p_misc[m][:, t * P:(t + 1) * P],
                                                          outT[g % OUT_BANKS][:, t * P:(t + 1) * P], w.ident[:])
                            ins.then_inc(misc_ready[m], 1)
                        elif kind == "AT":
                            m = take_misc()
                            if step[1] == 0:
                                wait_read(("OUT", 3))
                            for t in range(NT):
                                ins = nc.tensor.transpose(p_misc[m][:, t * P:(t + 1) * P],
                                                          attn[:, t, step[1] * P:(step[1] + 1) * P], w.ident[:])
                            ins.then_inc(misc_ready[m], 1)
                        elif kind == "WO":
                            m = take_misc()
                            if step[1] == 0:
                                wait_read(("AT", 1))
                            for s in range(2):
                                t = 2 * step[1] + s
                                for h in range(DC):
                                    ins = nc.tensor.matmul(p_misc[m][:, s * D:(s + 1) * D],
                                                           attnT[:, h, t * P:(t + 1) * P], wo[:, h, :],
                                                           start=(h == 0), stop=(h == DC - 1))
                            ins.then_inc(misc_ready[m], 1)
                        elif kind == "MAX":
                            m = take_misc()
                            e = step[1]
                            pe.wait_ge(smax_parts_ready, 2 * n + e + 1)
                            for t in range(NT):
                                ins = nc.tensor.transpose(p_misc[m][:, t * P // 2:(t + 1) * P // 2].bitcast(BF16),
                                                          smax_parts[e][:, t, :], ident16[:])
                            ins.then_inc(misc_ready[m], 1)
                        elif kind == "XT":
                            m = take_misc()
                            pe.wait_ge(xn_ready, j + 1)
                            for t in range(NT):
                                ins = nc.tensor.transpose(p_misc[m][:, t * P:(t + 1) * P],
                                                          x[:, t, step[1] * P:(step[1] + 1) * P], w.ident[:])
                            ins.then_inc(misc_ready[m], 1)
                        elif kind in ("Q", "LAT"):
                            weights = {"Q": wq, "LAT": w_down}[kind]
                            m = take_misc()
                            if step == ("LAT", 0):
                                wait_read(("XT", 1))
                            for h in range(DC):
                                ins = nc.tensor.matmul(p_misc[m][:], weights[:, h, step[1] * P:(step[1] + 1) * P],
                                                       xnT[:, h, :], start=(h == 0), stop=(h == DC - 1))
                            ins.then_inc(misc_ready[m], 1)
                        elif kind == "K":
                            m = take_misc()
                            if step == ("K", 0):
                                wait_read(("LAT", 0))
                            ins = nc.tensor.matmul(p_misc[m][:], wk[:, step[1] * P:(step[1] + 1) * P], latT[:],
                                                   start=True, stop=True)
                            ins.then_inc(misc_ready[m], 1)
                        elif kind == "V":
                            m = take_misc()
                            for s in range(2):
                                t = 2 * step[1] + s
                                ins = nc.tensor.matmul(p_misc[m][:, s * D:(s + 1) * D], latT[:, t * P:(t + 1) * P],
                                                       wv[:], start=True, stop=True)
                            ins.then_inc(misc_ready[m], 1)

                turns(pe, turn)


class Resident:
    pass


def load_resident(nc, ctx, dram):
    def sb(name, shape, dt=F32):
        return ctx.enter_context(nc.sbuf_tensor(name, shape, dt))

    w = Resident()
    w.gateT = sb("gateT", [P, DC, E])
    w.gate_b = sb("gate_b", [P, E])
    w.ident = sb("ident", [P, P])
    w.iota_slot = sb("iota_slot", [P, CAP], BF16)
    iota_slot_f = sb("iota_slot_f", [P, CAP])
    w.iota_expert = sb("iota_expert", [P, E])
    w.small = sb("small", [P, 8])
    w.lane = w.small[:, 0:1]
    w.dummy_row = w.small[:, 1:2]
    w.first_tiles = w.small[:, 4:8]
    w.minus_one = sb("minus_one", [P, NT])
    w.minus_half = sb("minus_half", [P, NT])
    w.eps = sb("eps", [P, NT])
    w.tiles_per_chunk = sb("tiles_per_chunk", [P, NT])
    w.before = sb("before", [P, P], BF16)
    w.ones = sb("ones", [P, P], BF16)
    w.ones_row = sb("ones_row", [P, T], BF16)
    w.slot_token = sb("slot_token", [P, E], I32)
    before_f = sb("before_f", [P, P])
    loaded = ctx.enter_context(nc.semaphore("resident_loaded"))
    wrote = ctx.enter_context(nc.semaphore("dummy_rows_written"))
    zeroed = ctx.enter_context(nc.semaphore("zeroed"))
    blank = sb("blank", [P, ROW])

    with nc.Block() as block:
        @block.sync
        def _(sp):
            n = 0
            for dst, src in ((w.gateT, dram.gateT), (w.gate_b, dram.gate_b), (w.ident, dram.ident), (w.small, dram.small),
                             (iota_slot_f, dram.iota_slot), (w.iota_expert, dram.iota_expert), (before_f, dram.before)):
                sp.dma_start(dst[:], src).then_inc(loaded, 16)
                n += 16
            sp.wait_ge(zeroed, 1)
            sp.dma_start(dram.rows[DUMMY:DUMMY + P, :], blank[:]).then_inc(wrote, 16)
            for a in dram.accs:
                sp.dma_start(a[DUMMY:DUMMY + P, :], blank[:, 0:D]).then_inc(wrote, 16)
            sp.wait_ge(loaded, n)
            sp.wait_ge(wrote, 16 * (1 + len(dram.accs)))

        @block.vector
        def _(dve):
            nc.vector.memset(blank[:], 0.0)
            nc.vector.memset(w.ones[:], 1.0)
            nc.vector.memset(w.minus_half[:], -0.5)
            nc.vector.memset(w.minus_one[:], -1.0)
            nc.vector.memset(w.eps[:], EPS)
            nc.vector.memset(w.tiles_per_chunk[:], float(NT))
            nc.vector.memset(w.ones_row[:], 1.0)
            dve.drain()
            dve.sem_inc(zeroed, 1)
            dve.wait_ge(loaded, 16 * 7)
            nc.vector.tensor_copy(w.before[:], before_f[:])
            nc.vector.tensor_copy(w.iota_slot[:], iota_slot_f[:])
    return w


class Dram:
    pass


def program(nc, dram):
    with ExitStack() as ctx:
        w = load_resident(nc, ctx, dram)
        route_and_share(nc, w, dram, dram.x_chunks, dram.acc1_chunks, "f1")
        experts(nc, w, dram, dram.accs[0], "e1")
        attention(nc, w, dram, dram.acc1_chunks, dram.mid, "a")
        route_and_share(nc, w, dram, dram.mid, dram.out_chunks, "f2")
        experts(nc, w, dram, dram.out_rows, "e2")


def kernel(**inputs):
    import numpy as np
    import concourse.bacc as bacc
    from concourse.bass_utils import run_bass_kernel_spmd

    nc = bacc.Bacc("TRN2", target_bir_lowering=False, num_devices=1)
    arrays = {}

    def put(name, a):
        a = np.ascontiguousarray(a)
        arrays[name] = a
        return nc.dram_tensor(name, a.shape, mybir.dt.from_np(a.dtype), kind="ExternalInput").ap()

    def halves(a):
        return a.reshape(2, P, -1).transpose(1, 0, 2)

    g = {k.removeprefix("L0_"): np.asarray(v) for k, v in inputs.items()}
    dram = Dram()
    chunked = "(c t p) d -> c p t d"
    dram.x_chunks = put("x_in", g["attn_x"].reshape(TOK, D)).rearrange(chunked, p=P, t=NT)
    dram.gateT = put("gateT_in", halves(g["ffn_gate_w"].T))
    dram.gate_b = put("gate_b_in", np.broadcast_to(g["ffn_gate_b"], (P, E)))
    dram.ws1T = put("ws1T_in", halves(g["ffn_ws1"].T))
    dram.ws3T = put("ws3T_in", halves(g["ffn_ws3"].T))
    dram.ws2T = put("ws2T_in", g["ffn_ws2"].T)
    w13 = np.concatenate([g["ffn_w1"], g["ffn_w3"]], axis=1)
    dram.w13 = put("w13_in", w13.transpose(0, 2, 1).reshape(E, DC, P, SI).transpose(0, 2, 1, 3))
    dram.w2 = put("w2_in", g["ffn_w2"].transpose(0, 2, 1).reshape(E, 2, IH, D).transpose(0, 2, 1, 3))
    lanes = np.arange(P, dtype=np.float32)
    dram.ident = put("ident_in", np.eye(P, dtype=np.float32))
    dram.before = put("before_in", np.triu(np.ones((P, P), np.float32), 1))
    dram.iota_slot = put("iota_slot_in", np.broadcast_to(lanes, (P, CAP)))
    dram.iota_expert = put("iota_expert_in", np.broadcast_to(lanes[:E], (P, E)))
    small = np.zeros((P, 8), np.float32)
    small[:, 0] = lanes
    small[:, 1] = DUMMY + P + lanes
    small[:, 4:8] = 1 + np.arange(NT) - NT
    dram.small = put("small_in", small)

    def scratch(name, shape, dt=F32):
        return nc.dram_tensor(name, shape, dt, kind="Internal").ap()

    dram.rows = scratch("rows", [TOK + P, ROW])
    dram.accs = [scratch(f"acc{n}", [TOK + P, D]) for n in range(1)]
    dram.rows_chunks = dram.rows[0:TOK, :].rearrange(chunked, p=P, t=NT)
    dram.acc1_chunks = dram.accs[0][0:TOK, :].rearrange(chunked, p=P, t=NT)
    dram.mid = scratch("mid", [TOK, D]).rearrange(chunked, p=P, t=NT)
    dram.wq = put("wq_in", halves(g["attn_wq"]))
    dram.w_down = put("w_down_in", halves(g["attn_w_down"]))
    dram.wk = put("wk_in", g["attn_wk_up"])
    dram.wv = put("wv_in", g["attn_wv_up"])
    dram.wo = put("wo_in", halves(g["attn_wo"]))
    inv = 1.0 / 10000.0 ** (np.arange(0, HD, 2, dtype=np.float32) / HD)
    angle = np.outer(np.arange(T, dtype=np.float32), inv)
    dram.cos = put("cos_in", np.tile(np.repeat(np.cos(angle).T, 2, axis=0), (P // HD, 1)).astype(np.float32))
    signed = np.stack([-np.sin(angle).T, np.sin(angle).T], axis=1).reshape(HD, T)
    dram.sin = put("sin_in", np.tile(signed, (P // HD, 1)).astype(np.float32))
    mask = np.zeros((MASK, 2 * T), np.float32)
    for t in range(NT):
        mask[t, t * P:t * P + PAGE] = 1
        mask[t, T + t * P + PAGE:T + (t + 1) * P] = -2.0 ** 60
    dram.mask = put("mask_in", mask)
    dram.parts = scratch("parts", [2, 2, 3, D, T], BF16)
    dram.smax = scratch("smax", [2, 2, TOP * H // 2, T], BF16)
    out = nc.dram_tensor("out", (TOK + P, D), F32, kind="ExternalOutput").ap()
    dram.out_rows = out
    dram.out_chunks = out[0:TOK, :].rearrange(chunked, p=P, t=NT)
    dram.accs.append(dram.out_rows)
    program(nc, dram)
    got = run_bass_kernel_spmd(nc, [arrays], core_ids=[0])
    return got.results[0]["out"][0:TOK].reshape(B, T, D)
```
